# Optimizing a Trainium2 kernel written in Bass

```python
import numpy as np
import jax
import jax.numpy as jnp

def _softmax(x, axis=-1):
    return jax.nn.softmax(x, axis=axis)

def _gelu(x):
    return jax.nn.gelu(x, approximate=True)

def _silu(x):
    return jax.nn.silu(x)

def _sigmoid(x):
    return jax.nn.sigmoid(x)

def _layernorm(x, axis=-1, eps=1e-05):
    m = jnp.mean(x, axis=axis, keepdims=True)
    v = jnp.var(x, axis=axis, keepdims=True)
    return (x - m) / jnp.sqrt(v + eps)

def _scatter_add(tgt, idx, src, axis=0):
    return tgt.at[idx].add(src)

def _segment_sum(src, seg, n):
    return jax.ops.segment_sum(src, seg, n)
kernel_name = 'mk_prb_d1_jaxref_r8_249ffe'

def setup_inputs(seed: int=0):
    np.random.seed(seed)
    _w = jnp.asarray

    def _L0_attn_setup():
        import jax, jax.numpy as jnp
        import numpy as np
        D_MODEL = 128
        D_STATE = 64
        D_CONV = 4
        EXPAND = 2
        HEADDIM = 128
        NGROUPS = 1
        D_INNER = EXPAND * D_MODEL
        NHEADS = D_INNER // HEADDIM
        CONV_DIM = D_INNER + 2 * NGROUPS * D_STATE
        D_IN_PROJ = 2 * D_INNER + 2 * NGROUPS * D_STATE + NHEADS
        BATCH, SEQLEN = (2, 256)
        DT_MIN, DT_MAX, DT_FLOOR = (0.001, 0.1, 0.0001)
        RMS_EPS = 1e-05

        def _mamba2_forward(u, in_proj_w, conv_w, conv_b, dt_bias, A_log, D_param, norm_w, out_proj_w):
            B, L, _ = u.shape
            zxbcdt = jnp.einsum('bld,ed->ble', u, in_proj_w)
            z = zxbcdt[..., :D_INNER]
            xBC = zxbcdt[..., D_INNER:D_INNER + CONV_DIM]
            dt = jax.nn.softplus(zxbcdt[..., D_INNER + CONV_DIM:] + dt_bias)
            xc = jnp.swapaxes(xBC, 1, 2)
            xc = jax.lax.conv_general_dilated(xc, conv_w, window_strides=(1,), padding=[(D_CONV - 1, 0)], feature_group_count=CONV_DIM)
            xc = jax.nn.silu(xc + conv_b[None, :, None])
            xBC = jnp.swapaxes(xc, 1, 2)
            x = xBC[..., :D_INNER].reshape(B, L, NHEADS, HEADDIM)
            Bmat = xBC[..., D_INNER:D_INNER + D_STATE]
            Cmat = xBC[..., D_INNER + D_STATE:]
            A = -jnp.exp(A_log)

            def step(state, inp):
                dt_t, x_t, B_t, C_t = inp
                dA = jnp.exp(dt_t * A)[:, :, None, None]
                state = state * dA + dt_t[:, :, None, None] * x_t[:, :, :, None] * B_t[:, None, None, :]
                y_t = jnp.einsum('bhpn,bn->bhp', state, C_t) + D_param[None, :, None] * x_t
                return (state, y_t)
            state0 = jnp.zeros((B, NHEADS, HEADDIM, D_STATE), u.dtype)
            inputs = (jnp.moveaxis(dt, 1, 0), jnp.moveaxis(x, 1, 0), jnp.moveaxis(Bmat, 1, 0), jnp.moveaxis(Cmat, 1, 0))
            _, ys = jax.lax.scan(step, state0, inputs)
            y = jnp.moveaxis(ys, 0, 1).reshape(B, L, D_INNER)
            yg = y * jax.nn.silu(z)
            rms = jax.lax.rsqrt(jnp.mean(yg * yg, axis=-1, keepdims=True) + RMS_EPS)
            yn = yg * rms * norm_w
            return jnp.einsum('ble,de->bld', yn, out_proj_w)
        key = jax.random.key(seed)
        ks = jax.random.split(key, 8)
        u = jax.random.normal(ks[0], (BATCH, SEQLEN, D_MODEL), jnp.float32)
        in_proj_w = jax.random.normal(ks[1], (D_IN_PROJ, D_MODEL), jnp.float32) * 0.02
        conv_w = jax.random.normal(ks[2], (CONV_DIM, 1, D_CONV), jnp.float32) * 0.2
        conv_b = jax.random.normal(ks[3], (CONV_DIM,), jnp.float32) * 0.02
        dt = jnp.exp(jax.random.uniform(ks[4], (NHEADS,)) * (jnp.log(DT_MAX) - jnp.log(DT_MIN)) + jnp.log(DT_MIN))
        dt = jnp.maximum(dt, DT_FLOOR)
        dt_bias = dt + jnp.log(-jnp.expm1(-dt))
        A_log = jnp.log(jax.random.uniform(ks[5], (NHEADS,), minval=1.0, maxval=16.0))
        D_param = jnp.ones((NHEADS,), jnp.float32)
        norm_w = jnp.ones((D_INNER,), jnp.float32)
        out_proj_w = jax.random.normal(ks[6], (D_MODEL, D_INNER), jnp.float32) * 0.02
        return {'u': u, 'in_proj_w': in_proj_w, 'conv_w': conv_w, 'conv_b': conv_b, 'dt_bias': dt_bias, 'A_log': A_log, 'D_param': D_param, 'norm_w': norm_w, 'out_proj_w': out_proj_w}
    _L0_attn_in = _L0_attn_setup()

    def _L0_ffn_setup():
        import jax, jax.numpy as jnp
        import numpy as np
        N_EMBED = 128
        HIDDEN = int(2 / 3 * 4 * N_EMBED)
        NUM_EXPERTS = 8
        TOP_K = 2
        key = jax.random.key(seed)
        ks = jax.random.split(key, 5)
        B, T, C, E, H = (2, 256, N_EMBED, NUM_EXPERTS, HIDDEN)
        s = 0.02
        return {'x': jax.random.normal(ks[0], (B, T, C), dtype=jnp.float32), 'gate_w': jax.random.normal(ks[1], (E, C), dtype=jnp.float32) * s, 'w1': jax.random.normal(ks[2], (E, H, C), dtype=jnp.float32) * s, 'w2': jax.random.normal(ks[3], (E, H, C), dtype=jnp.float32) * s, 'w3': jax.random.normal(ks[4], (E, C, H), dtype=jnp.float32) * s}
    _L0_ffn_in = _L0_ffn_setup()
    _d = {'L0_attn_u': _L0_attn_in['u'], 'L0_attn_in_proj_w': _L0_attn_in['in_proj_w'], 'L0_attn_conv_w': _L0_attn_in['conv_w'], 'L0_attn_conv_b': _L0_attn_in['conv_b'], 'L0_attn_dt_bias': _L0_attn_in['dt_bias'], 'L0_attn_A_log': _L0_attn_in['A_log'], 'L0_attn_D_param': _L0_attn_in['D_param'], 'L0_attn_norm_w': _L0_attn_in['norm_w'], 'L0_attn_out_proj_w': _L0_attn_in['out_proj_w'], 'L0_ffn_gate_w': _L0_ffn_in['gate_w'], 'L0_ffn_w1': _L0_ffn_in['w1'], 'L0_ffn_w2': _L0_ffn_in['w2'], 'L0_ffn_w3': _L0_ffn_in['w3']}
    _x0 = _d['L0_attn_u']
    _d['L0_attn_u'] = jax.random.normal(jax.random.fold_in(jax.random.key(seed), 1), (2, 2048, 128), dtype=_x0.dtype)
    del _x0
    return _d

def reference(L0_attn_u, L0_attn_in_proj_w, L0_attn_conv_w, L0_attn_conv_b, L0_attn_dt_bias, L0_attn_A_log, L0_attn_D_param, L0_attn_norm_w, L0_attn_out_proj_w, L0_ffn_gate_w, L0_ffn_w1, L0_ffn_w2, L0_ffn_w3):

    def _L0_attn_ref(u, in_proj_w, conv_w, conv_b, dt_bias, A_log, D_param, norm_w, out_proj_w):
        import jax, jax.numpy as jnp
        import numpy as np
        D_MODEL = 128
        D_STATE = 64
        D_CONV = 4
        EXPAND = 2
        HEADDIM = 128
        NGROUPS = 1
        D_INNER = EXPAND * D_MODEL
        NHEADS = D_INNER // HEADDIM
        CONV_DIM = D_INNER + 2 * NGROUPS * D_STATE
        D_IN_PROJ = 2 * D_INNER + 2 * NGROUPS * D_STATE + NHEADS
        BATCH, SEQLEN = (2, 256)
        DT_MIN, DT_MAX, DT_FLOOR = (0.001, 0.1, 0.0001)
        RMS_EPS = 1e-05

        def _mamba2_forward(u, in_proj_w, conv_w, conv_b, dt_bias, A_log, D_param, norm_w, out_proj_w):
            B, L, _ = u.shape
            zxbcdt = jnp.einsum('bld,ed->ble', u, in_proj_w)
            z = zxbcdt[..., :D_INNER]
            xBC = zxbcdt[..., D_INNER:D_INNER + CONV_DIM]
            dt = jax.nn.softplus(zxbcdt[..., D_INNER + CONV_DIM:] + dt_bias)
            xc = jnp.swapaxes(xBC, 1, 2)
            xc = jax.lax.conv_general_dilated(xc, conv_w, window_strides=(1,), padding=[(D_CONV - 1, 0)], feature_group_count=CONV_DIM)
            xc = jax.nn.silu(xc + conv_b[None, :, None])
            xBC = jnp.swapaxes(xc, 1, 2)
            x = xBC[..., :D_INNER].reshape(B, L, NHEADS, HEADDIM)
            Bmat = xBC[..., D_INNER:D_INNER + D_STATE]
            Cmat = xBC[..., D_INNER + D_STATE:]
            A = -jnp.exp(A_log)

            def step(state, inp):
                dt_t, x_t, B_t, C_t = inp
                dA = jnp.exp(dt_t * A)[:, :, None, None]
                state = state * dA + dt_t[:, :, None, None] * x_t[:, :, :, None] * B_t[:, None, None, :]
                y_t = jnp.einsum('bhpn,bn->bhp', state, C_t) + D_param[None, :, None] * x_t
                return (state, y_t)
            state0 = jnp.zeros((B, NHEADS, HEADDIM, D_STATE), u.dtype)
            inputs = (jnp.moveaxis(dt, 1, 0), jnp.moveaxis(x, 1, 0), jnp.moveaxis(Bmat, 1, 0), jnp.moveaxis(Cmat, 1, 0))
            _, ys = jax.lax.scan(step, state0, inputs)
            y = jnp.moveaxis(ys, 0, 1).reshape(B, L, D_INNER)
            yg = y * jax.nn.silu(z)
            rms = jax.lax.rsqrt(jnp.mean(yg * yg, axis=-1, keepdims=True) + RMS_EPS)
            yn = yg * rms * norm_w
            return jnp.einsum('ble,de->bld', yn, out_proj_w)
        return _mamba2_forward(u, in_proj_w, conv_w, conv_b, dt_bias, A_log, D_param, norm_w, out_proj_w)

    def _L0_ffn_ref(x, gate_w, w1, w2, w3):
        import jax, jax.numpy as jnp
        import numpy as np
        N_EMBED = 128
        HIDDEN = int(2 / 3 * 4 * N_EMBED)
        NUM_EXPERTS = 8
        TOP_K = 2
        B, T, C = x.shape
        E = gate_w.shape[0]
        xt = x.reshape(-1, C)
        N = xt.shape[0]
        logits = jnp.einsum('nc,ec->ne', xt, gate_w)
        top_vals, top_idx = jax.lax.top_k(logits, TOP_K)
        top_w = jax.nn.softmax(top_vals.astype(jnp.float32), axis=-1).astype(x.dtype)
        route = jnp.zeros((N, E), dtype=x.dtype)
        route = route.at[jnp.arange(N)[:, None], top_idx].set(top_w)
        h1 = jnp.einsum('nc,ehc->enh', xt, w1)
        h2 = jnp.einsum('nc,ehc->enh', xt, w2)
        act = jax.nn.silu(h1) * h2
        expert_out = jnp.einsum('enh,ech->enc', act, w3)
        out = jnp.einsum('ne,enc->nc', route, expert_out)
        return out.reshape(B, T, C)
    x = L0_attn_u
    xn = _layernorm(x, axis=-1)
    x = x + _L0_attn_ref(xn, L0_attn_in_proj_w, L0_attn_conv_w, L0_attn_conv_b, L0_attn_dt_bias, L0_attn_A_log, L0_attn_D_param, L0_attn_norm_w, L0_attn_out_proj_w) + _L0_ffn_ref(xn, L0_ffn_gate_w, L0_ffn_w1, L0_ffn_w2, L0_ffn_w3)
    return x

_drawn_inputs = setup_inputs


def setup_inputs(seed=0):
    import zlib

    import numpy as np

    out = dict(_drawn_inputs(seed))
    spreads = {'L0_attn_D_param': (1.0, 0.6), 'L0_attn_norm_w': (1.0, 0.6)}
    factors = {'L0_attn_dt_bias': 8.0,
     'L0_attn_A_log': 8.0,
     'L0_ffn_gate_w': 8.0,
     'L0_ffn_w1': 8.0,
     'L0_ffn_w2': 8.0,
     'L0_ffn_w3': 8.0,
     'L0_attn_conv_b': 4.535}
    for name, (base, spread) in spreads.items():
        noise = np.random.default_rng([zlib.crc32(name.encode()), seed]).standard_normal(out[name].shape)
        drawn = base * np.exp(spread * noise) if base else spread * noise
        out[name] = jnp.asarray(drawn.astype(out[name].dtype))
    for name, factor in factors.items():
        out[name] = (out[name] * factor).astype(out[name].dtype)
    return out
```

```python
from contextlib import ExitStack

import concourse.bass as bass
from concourse import mybir

F32 = mybir.dt.float32
U32 = mybir.dt.uint32
I32 = mybir.dt.int32
ALU = mybir.AluOpType
ACT = mybir.ActivationFunctionType
AX = mybir.AxisListType

P = 128
LN_EPS = 1e-5
RMS_EPS = 1e-5
DECAY_FLOOR = -104.0
TOP_K = 2
OOB = 65535


def rolled(eng, n, head, tail, unroll, body, done=0):
    first = -(-head // unroll)
    last = (n - tail) // unroll
    for s in range(done, first * unroll):
        body(s // unroll, s % unroll)
    with eng.Fori(first, last, 1) as g:
        for u in range(unroll):
            body(g, u)
    for s in range(last * unroll, n):
        body(s // unroll, s % unroll)


def fixed(i):
    return isinstance(i, int)


def from_(i, k):
    return not fixed(i) or i >= k


def before(i, n):
    return not fixed(i) or i < n


def build(nc, u, in_projT, conv_w, conv_b, dt_bias, A_log, D_param, norm_w, out_projT, gateT, w1T, w2T, w3T, out):
    BATCH, SEQ, D = u.shape
    N = BATCH * SEQ
    TILES = N // P
    Q = 4
    KC = Q // BATCH
    QUADS = TILES // Q
    E, HID = w1T.shape[1], w1T.shape[2]
    DI = norm_w.shape[0] * norm_w.shape[1]
    HEADS = dt_bias.shape[0]
    CONV = conv_b.shape[0] * conv_b.shape[1]
    TAPS = conv_w.shape[2]
    DS = (CONV - DI) // 2
    CT = CONV // P
    HALO = TAPS - 1
    W = Q * P
    SL_ = KC * P
    NL = E + HEADS
    HC = -(-HID // P)
    BLOCKS = (N * TOP_K) // P + E
    ROW = D + 2
    R8 = 8
    assert D == P and HEADS == 2 and DI == HEADS * P and DS == 64 and BLOCKS % R8 == 0 and CT == 3

    with ExitStack() as ctx:
        def sb(name, shape, dt=F32):
            return ctx.enter_context(nc.sbuf_tensor(name, shape, dt))

        def sem(name):
            return ctx.enter_context(nc.semaphore(name))

        def sems(name, n):
            return [sem(f"{name}{k}") for k in range(n)]

        sorted_rows = nc.dram_tensor("sorted_rows", [BLOCKS * P, ROW], F32, kind="Internal").ap()
        slot_rows = nc.dram_tensor("slot_rows", [N * TOP_K, D], F32, kind="Internal").ap()
        ecum_rows = nc.dram_tensor("ecum_rows", [TILES * HEADS, P], F32, kind="Internal").ap()

        ident = sb("ident", [P, P])
        upper = sb("upper", [P, P])
        after = sb("after", [P, P])
        earlier = sb("earlier", [P, P])
        ones = sb("ones", [P, P])
        neg_half = sb("neg_half", [P, Q])
        eps_c = sb("eps_c", [P, Q])
        minus_c = sb("minus_c", [P, Q])
        rank_e = sb("rank_e", [P, TILES, E])
        block_edge = sb("block_edge", [P, TILES])
        block_no = sb("block_no", [1, BLOCKS])
        w_in = sb("w_in", [P, 2 * DI + 2 * DS + HEADS])
        w_small = sb("w_small", [P, NL])
        w_conv = sb("w_conv", [P, CT, TAPS])
        b_conv = sb("b_conv", [P, CT])
        b_dt = sb("b_dt", [P, HEADS])
        neg_a = sb("neg_a", [P, HEADS])
        a_log = sb("a_log", [P, HEADS])
        d_skip = sb("d_skip", [P, HEADS])
        w_norm = sb("w_norm", [P, HEADS])
        w_out = sb("w_out", [P, HEADS, D])
        w12 = sb("w12", [P, E * 2 * HID])
        w3 = sb("w3", [P, E * HC * D])
        w3v = w3[:, :].rearrange("p (e k c) -> p e k c", e=E, k=HC)

        acc = sb("acc", [P, TILES, D])
        xnT = sb("xnT", [P, TILES * P])
        rows = sb("rows", [P, TOP_K, TILES, ROW])
        dest = sb("dest", [P, TOP_K, TILES], U32)
        dt_all = sb("dt_all", [P, TILES, HEADS])
        a_all = sb("a_all", [P, TILES, HEADS])
        w_end = sb("w_end", [P, TILES, HEADS])
        e_tot = sb("e_tot", [P, TILES])
        expert_off = sb("expert_off", [1, 2, BLOCKS], I32)
        state = [[sb(f"state{b}{k}", [P, P]) for k in range(2)] for b in range(BATCH)]

        WORK = 23 * 1024
        work = sb("work", [P, WORK])
        used = [0]

        def carve(shape, dt=F32):
            n = 1
            for s in shape:
                n *= s
            a = work[:, used[0]:used[0] + n]
            used[0] += n
            assert used[0] <= WORK, used[0]
            if dt is not F32:
                a = a.bitcast(dt)
            if len(shape) == 1:
                return a
            names = "abcd"[:len(shape)]
            return a.rearrange(f"p ({' '.join(names)}) -> p {' '.join(names)}",
                               **{names[k]: shape[k] for k in range(1, len(shape))})

        pre = [carve([CT, BATCH, HALO + SL_]) for _ in range(2)]
        conv = carve([CT, W])
        xT = [carve([HEADS, W]) for _ in range(2)]
        bcT = [carve([W]) for _ in range(2)]
        zs = [carve([HEADS, W]) for _ in range(2)]
        split = used[0]
        xn = [carve([Q, D]) for _ in range(2)]
        xnTs = [carve([W]) for _ in range(2)]
        stats = [carve([Q, 6]) for _ in range(2)]
        mean_var = [carve([Q, 2]) for _ in range(2)]
        ve = [carve([Q]) for _ in range(2)]
        rstd = [carve([Q]) for _ in range(2)]
        nmean = [carve([Q]) for _ in range(2)]
        nbias = [carve([Q]) for _ in range(2)]
        FILL = 8
        fill = carve([FILL, ROW])
        lg = carve([TILES, NL])
        V = [carve([TILES, E]) for _ in range(4)]
        VT = [carve([E, TILES]) for _ in range(5)]
        hot = [carve([TILES, E]) for _ in range(2)]
        tn = [carve([TILES]) for _ in range(6)]
        ex_top = carve([TILES])
        en = [carve([E]) for _ in range(6)]
        be = carve([BLOCKS, E])
        bn = carve([BLOCKS])
        sp_ = [carve([TILES, HEADS]) for _ in range(10)]
        minus1 = carve([TILES, HEADS])
        ecum = carve([TILES, HEADS])
        ecT = carve([P])
        used[0] = split
        xdt = [carve([Q, HEADS, P]) for _ in range(2)]
        bw = carve([Q, HEADS, DS])
        gT = carve([W])
        mT = [carve([W]) for _ in range(HEADS)]
        ed = [carve([W]) for _ in range(HEADS)]
        cd = [carve([W]) for _ in range(2)]
        ce = carve([W])
        ebc = [carve([Q, P]) for _ in range(2)]
        aU = carve([HEADS, W])
        yg = carve([HEADS, W])
        sq = carve([HEADS, W])
        ms = [carve([Q]) for _ in range(2)]
        rms = [carve([Q]) for _ in range(2)]
        used[0] = 0
        xin = [carve([ROW]) for _ in range(R8)]
        xg = [carve([P]) for _ in range(2)]
        s1 = [carve([HID + HID % 2]) for _ in range(2)]
        am = [carve([HC * P]) for _ in range(2)]
        amT = [carve([HC * P]) for _ in range(2)]
        yo = [carve([D]) for _ in range(R8)]
        ys = [carve([Q, TOP_K, D]) for _ in range(2)]
        res = [carve([Q, D]) for _ in range(2)]

        bank = [ctx.enter_context(nc.psum_tensor(f"bank{k}", [P, 512], F32)) for k in range(8)]

        wts_route = sem("router_weights_in")
        wts = sem("weights_in")
        wts_moe = sem("expert_weights_in")
        c_one = sem("constant_filled")
        c_done = sem("constants_ready")
        f_set = sem("fill_ready")
        f_meta = sem("fill_meta")
        f_out = sem("list_filled")
        s_zero = sem("states_zeroed")
        w3_zero = sem("w3_zeroed")
        x_in = sems("x_in", 2)
        a_stats, a_mv, a_ve, a_rstd, a_nb, a_norm, a_row, a_tr, a_cpT, a_cpTs, a_lg = (
            sem(n) for n in ("ln_stats", "ln_mean_var", "ln_ve", "ln_rstd", "ln_bias", "ln_normed", "ln_rows",
                             "ln_transposed", "xnT_ready", "xnTs_ready", "logits_ready"))
        v_link = sem("vector_step")
        g_link = sem("gpsimd_step")
        r_lg = sem("logits_copied")
        r_d = sem("top_gap_ready")
        r_ex = sem("top_exp_ready")
        r_mask = sem("route_mask_ready")
        r_cnt = sem("route_counts_ready")
        r_dest = sem("destinations_ready")
        r_off = sem("expert_offsets_ready")
        r_abs = sem("dt_abs_ready")
        r_exp = sem("dt_exp_ready")
        r_na = sem("exp_a_log_ready")
        r_a = sem("decays_ready")
        r_cum = sem("cumulated_ready")
        r_ecum = sem("ecum_ready")
        r_tot = sem("chunk_decays_ready")
        r_ecT = sem("ecum_transposed")
        r_ecS = sem("ecum_copied")
        r_ecD = sem("ecum_stored")
        r_wo = sem("w_out_ready")
        sc_in = sem("rows_scattered")
        p_pre, p_z, p_T, p_G, p_D, p_st, p_y, p_O = (
            sem(n) for n in ("conv_in_projected", "z_projected", "x_transposed", "bc_product", "decay_sums",
                             "state_added", "y_ready", "out_projected"))
        s_pre, s_z, s_xs, s_ed, s_sq = (sem(n) for n in ("pre_copied", "z_silued", "conv_silued", "decays_exped",
                                                         "squares_ready"))
        v_halo, v_tap, v_conv, v_xdt, v_bw, v_gT, v_mT, v_ce, v_S, v_ye, v_yg, v_ms, v_out, v_aU = (
            sem(n) for n in ("halo_copied", "tap_added", "conv_ready", "xdt_ready", "bw_ready", "gT_ready",
                             "mT_ready", "ce_ready", "state_ready", "y_skip_added", "y_gated", "mean_square_ready",
                             "mamba_added", "aU_ready"))
        g_rms = sem("rms_ready")
        e_in = sems("ecum_in", 2)
        c_in = sems("c_copied", 2)
        m_in = sems("block_in", R8)
        m_pad = sem("pad_zeroed")
        m_T, m_h1, m_h2, m_ta, m_o = (sem(n) for n in ("rows_transposed", "h1_ready", "h2_ready",
                                                       "act_transposed", "expert_out_ready"))
        m_xg, m_s, m_a, m_aT, m_yo = (sem(n) for n in ("rowsT_ready", "silu_ready", "act_ready", "actT_ready",
                                                       "expert_rows_ready"))
        m_out = sems("expert_rows_out", R8)
        y_in = sems("slots_in", 2)
        f_sum, f_res = sem("slots_summed"), sem("result_ready")
        o_out = sems("result_out", 2)

        block = ctx.enter_context(nc.Block())

        def tiles_view(dram):
            return dram.rearrange("b (i k p) d -> i p b k d", k=KC, p=P)

        u_v, out_v = tiles_view(u), tiles_view(out)
        slots_v = slot_rows.rearrange("(b i k p s) d -> i p b k (s d)", b=BATCH, k=KC, p=P, s=TOP_K)
        ecum_v = ecum_rows.rearrange("(i m h) t -> i h m t", m=Q, h=HEADS)
        sorted_v = sorted_rows.rearrange("(n p) r -> n p r", p=P)

        def quad(t, i):
            return t[:, bass.ds(Q * i, Q)]

        def take_over_b(eng):
            eng.wait_ge(a_row, TOP_K * QUADS)
            eng.wait_ge(f_out, 16 * BLOCKS // FILL)
            eng.wait_ge(r_ecD, 16)
            eng.wait_ge(r_off, 1)

        @block.sync
        def _(sp):
            def load_x(g, w):
                i = 2 * g + w
                if from_(i, 2):
                    sp.wait_ge(a_stats, i - 1)
                for b in range(BATCH):
                    sp.dma_start(acc[:, bass.ds(Q * i + KC * b, KC), :],
                                 u_v[i][:, b]).then_inc(x_in[w], 16)
                if fixed(i) and i == 1:
                    small_weights()

            def small_weights():
                sp.dma_start(w_small[:, 0:E], gateT).then_inc(wts_route, 16)
                sp.dma_start(w_small[:, E:NL], in_projT[:, 2 * DI + 2 * DS:]).then_inc(wts_route, 16)
                sp.dma_start(b_dt[:, :], dt_bias.partition_broadcast(P)).then_inc(wts, 16)
                sp.dma_start(a_log[:, :], A_log.partition_broadcast(P)).then_inc(wts, 16)
                sp.dma_start(d_skip[:, :], D_param.partition_broadcast(P)).then_inc(wts, 16)
                sp.dma_start(w_norm[:, :], norm_w).then_inc(wts, 16)
                sp.dma_start(b_conv[:, :], conv_b).then_inc(wts, 16)
                sp.dma_start(w_conv[:, :, :], conv_w).then_inc(wts, 16)
                sp.dma_start(w_out[:, :, :], out_projT.rearrange("(h p) d -> p h d", p=P)).then_inc(wts, 16)
                sp.dma_start(w_in[:, :], in_projT).then_inc(wts, 16)

            rolled(sp, QUADS, 2, 0, 2, load_x)
            sp.wait_ge(f_set, 1)
            sp.wait_ge(f_meta, 1)
            fv = sorted_rows.rearrange("(p c q) r -> c p (q r)", p=P, q=FILL)
            for c in range(BLOCKS // FILL):
                sp.dma_start(fv[c], fill.rearrange("p q r -> p (q r)")).then_inc(f_out, 16)
            v12 = w12[:, :].rearrange("p (e two h) -> p e two h", e=E, two=2)
            sp.dma_start(v12[:, :, 0, :], w1T).then_inc(wts_moe, 16)
            sp.dma_start(v12[:, :, 1, :], w2T).then_inc(wts_moe, 16)
            sp.wait_ge(w3_zero, 1)
            for k in range(HC):
                m = min(P, HID - k * P)
                sp.dma_start(w3v[0:m, :, k, :], w3T[k * P:k * P + m]).then_inc(wts_moe, 16)
            sp.wait_ge(r_ecS, 1)
            sp.dma_start(ecum_rows, ecT[0:TILES * HEADS, :]).then_inc(r_ecD, 16)

            take_over_b(sp)

            def feed(g, w):
                i = 2 * g + w
                if from_(i, 2):
                    sp.wait_ge(v_ce, i - 1)
                src = ecum_v[i]
                for h in range(HEADS):
                    sp.dma_start(ebc[w][DS * h:DS * h + DS],
                                 src[h].partition_broadcast(DS)).then_inc(e_in[w], 16)
                sp.wait_ge(s_xs, 3 * i + 3)
                if from_(i, 2):
                    sp.wait_ge(p_G, i - 1)
                for h in range(HEADS):
                    sp.dma_start(cd[w][DS * h:DS * h + DS, :], bcT[w][DS:2 * DS, :]).then_inc(c_in[w], 16)

            rolled(sp, QUADS, 2, 0, 2, feed)

            sp.wait_ge(sc_in, 16 * TOP_K * TILES)
            sp.wait_ge(v_out, QUADS)
            sp.wait_ge(p_O, QUADS)

            def load_block(g, w):
                if from_(g, 1):
                    sp.wait_ge(m_out[w], 16 * g)
                j = R8 * g + w
                sp.dma_start(xin[w], sorted_v[j]).then_inc(m_in[w], 16)

            rolled(sp, BLOCKS, R8, 0, R8, load_block)

            for w in range(R8):
                sp.wait_ge(m_out[w], 16 * (BLOCKS // R8))

            def store(g, w):
                i = 2 * g + w
                sp.wait_ge(f_res, i + 1)
                for b in range(BATCH):
                    sp.dma_start(out_v[i][:, b], res[w][:, KC * b:KC * b + KC, :]).then_inc(o_out[w], 16)

            def fetch(g, w):
                i = 2 * g + w
                if from_(i, 2):
                    sp.wait_ge(f_sum, i - 1)
                for b in range(BATCH):
                    sp.dma_start(ys[w][:, KC * b:KC * b + KC].rearrange("p k s d -> p k (s d)"),
                                 slots_v[i][:, b]).then_inc(y_in[w], 16)
                if from_(i, 2):
                    store(g - 1, w)

            rolled(sp, QUADS, 2, 0, 2, fetch)
            for w in range(2):
                store(QUADS // 2 - 1, w)
            for w in range(2):
                sp.wait_ge(o_out[w], 16 * BATCH * QUADS // 2)

        @block.gpsimd
        def _(gp):
            def tri(t, pattern, cm, op):
                gp.affine_select(out=t[:, :], in_=t[:, :], compare_op=op, fill=0.0, base=0,
                                 pattern=[[pattern, P]], channel_multiplier=cm).then_inc(c_done, 1)

            gp.memset(ident[:, :], 0.0).then_inc(c_one, 1)
            for t in (upper, after, earlier):
                gp.memset(t[:, :], 1.0).then_inc(c_one, 1)
            gp.wait_ge(c_one, 4)
            gp.affine_select(out=ident[:, :], in_=ident[:, :], compare_op=ALU.not_equal, fill=1.0, base=0,
                             pattern=[[-1, P]], channel_multiplier=1).then_inc(c_done, 1)
            gp.memset(neg_half[:, :], -0.5).then_inc(c_done, 1)
            gp.memset(eps_c[:, :], LN_EPS).then_inc(c_done, 1)
            gp.memset(minus_c[:, :], -1.0).then_inc(c_done, 1)
            tri(upper, 1, -1, ALU.is_ge)
            tri(after, -1, 1, ALU.is_gt)
            tri(earlier, 1, -1, ALU.is_gt)
            gp.memset(ones[:, :], 1.0).then_inc(c_done, 1)

            gp.iota(rank_e[:, :, :], [[0, TILES], [-1, E]], base=E, channel_multiplier=0,
                    allow_small_or_imprecise_dtypes=True).then_inc(c_done, 1)
            gp.iota(block_edge[:, :], [[P, TILES]], base=0, channel_multiplier=0,
                    allow_small_or_imprecise_dtypes=True).then_inc(c_done, 1)
            gp.iota(block_no[:, :], [[1, BLOCKS]], base=0, channel_multiplier=0,
                    allow_small_or_imprecise_dtypes=True).then_inc(c_done, 1)
            for s in range(TOP_K):
                for b in range(BATCH):
                    gp.iota(rows[:, s].bitcast(U32).rearrange("p (i b k) r -> p b i k r", b=BATCH, k=KC)
                            [:, b, :, :, D + 1],
                            [[TOP_K * KC * P, QUADS], [TOP_K * P, KC]], base=TOP_K * SEQ * b + s,
                            channel_multiplier=TOP_K).then_inc(c_done, 1)

            def ln(g, w):
                i = 2 * g + w
                if True:
                    gp.wait_ge(a_mv, i + 1)
                    if from_(i, 2):
                        gp.wait_ge(a_norm, i - 1)
                    gp.tensor_tensor(ve[w], mean_var[w][:, :, 1], eps_c[:, :], ALU.add).then_inc(a_ve, 1)
                    gp.tensor_tensor(nmean[w], mean_var[w][:, :, 0], minus_c[:, :], ALU.mult).then_inc(a_ve, 1)
                    gp.wait_ge(a_ve, 2 * i + 2)
                    gp.tensor_tensor(rstd[w], ve[w], neg_half[:, :], ALU.pow).then_inc(a_rstd, 1)
                    gp.wait_ge(a_rstd, i + 1)
                    gp.tensor_tensor(nbias[w], nmean[w], rstd[w], ALU.mult).then_inc(a_nb, 1)

            gp.wait_ge(c_done, 11 + TOP_K * BATCH)
            rolled(gp, QUADS, 2, 0, 2, ln)

            steps = [0]

            def link(ins):
                steps[0] += 1
                ins.then_inc(g_link, 1)
                gp.wait_ge(g_link, steps[0])

            def wide2(t):
                return t.unsqueeze(1).to_broadcast([P, TILES, HEADS])

            gp.wait_ge(r_lg, 1)
            gp.wait_ge(wts, 128)
            x, relu, twice, mag, e, den, inv, s_, s2, poly = sp_
            link(gp.tensor_tensor(x, lg[:, :, E:NL], wide2(b_dt[:, :]), ALU.add))
            link(gp.tensor_scalar(relu, x, 0.0, None, ALU.max))
            link(gp.tensor_tensor(twice, relu, relu, ALU.add))
            gp.tensor_tensor(mag, twice, x, ALU.subtract).then_inc(r_abs, 1)
            gp.wait_ge(r_na, 1)
            link(gp.tensor_scalar(neg_a[:, :], neg_a[:, :], -1.0, None, ALU.mult))
            gp.memset(minus1, -1.0).then_inc(g_link, 1)
            steps[0] += 1
            gp.wait_ge(r_exp, 1)
            link(gp.tensor_scalar(den, e, 2.0, None, ALU.add))
            link(gp.tensor_tensor(inv, den, minus1, ALU.pow))
            link(gp.tensor_tensor(s_, e, inv, ALU.mult))
            link(gp.tensor_tensor(s2, s_, s_, ALU.mult))
            link(gp.tensor_scalar(poly, s2, 1.0 / 15, 1.0 / 13, ALU.mult, ALU.add))
            for c in (11, 9, 7, 5, 3, 1):
                link(gp.tensor_tensor(poly, poly, s2, ALU.mult))
                link(gp.tensor_scalar(poly, poly, 1.0, 1.0 / c, ALU.mult, ALU.add))
            link(gp.tensor_tensor(poly, poly, s_, ALU.mult))
            link(gp.tensor_tensor(poly, poly, poly, ALU.add))
            link(gp.tensor_tensor(dt_all[:, :, :], poly, relu, ALU.add))
            link(gp.tensor_tensor(inv, dt_all[:, :, :], wide2(neg_a[:, :]), ALU.mult))
            gp.tensor_scalar(a_all[:, :, :], inv, DECAY_FLOOR, None, ALU.max).then_inc(r_a, 1)

            gp.wait_ge(f_out, 16 * BLOCKS // FILL)
            gp.wait_ge(r_dest, 1)
            gp.wait_ge(a_row, TOP_K * QUADS)

            def scatter(i):
                for s in range(TOP_K):
                    for m in range(Q):
                        r = Q * i + m
                        gp.indirect_dma_start(
                            out=sorted_rows, out_offset=bass.IndirectOffsetOnAxis(ap=dest[:, s, r:r + 1], axis=0),
                            in_=rows[:, s, r, :], in_offset=None).then_inc(sc_in, 16)

            for i in range(QUADS):
                scatter(i)
                gp.wait_ge(v_ms, i + 1)
                if i >= 2:
                    gp.wait_ge(v_out, i - 1)
                gp.tensor_tensor(rms[i % 2], ms[i % 2], neg_half[:, :], ALU.pow).then_inc(g_rms, 1)

            bound = gp.to_reg(N * TOP_K - 1)

            def put(g, w):
                gp.wait_ge(m_yo, R8 * g + w + 1)
                gp.wait_ge(m_in[w], 16 * (g + 1))
                gp.indirect_dma_start(
                    out=slot_rows, out_offset=bass.IndirectOffsetOnAxis(ap=xin[w][:, D + 1:D + 2].bitcast(U32), axis=0),
                    in_=yo[w], in_offset=None, bounds_check=bound, oob_is_err=False).then_inc(m_out[w], 16)

            for j in range(BLOCKS):
                put(j // R8, j % R8)

        @block.scalar
        def _(act):
            def norm(g, w):
                i = 2 * g + w
                if from_(i, 2):
                    act.wait_ge(a_tr, i - 1)
                    act.activation(xnT[:, bass.ds(W * (i - 2), W)], bank[w][:, :], ACT.Copy).then_inc(a_cpT, 1)
                if before(i, QUADS):
                    act.wait_ge(a_nb, i + 1)
                    if from_(i, 2):
                        act.wait_ge(a_row, TOP_K * (i - 1))
                    for m in range(Q):
                        n = act.activation(xn[w][:, m, :], acc[:, Q * i + m, :],
                                           ACT.Identity, bias=nbias[w][:, m:m + 1], scale=rstd[w][:, m:m + 1])
                    n.then_inc(a_norm, 1)

            rolled(act, QUADS + 2, 2, 2, 2, norm)
            act.wait_ge(wts, 128)
            act.activation(neg_a[:, :], a_log[:, :], ACT.Exp).then_inc(r_na, 1)
            act.wait_ge(r_abs, 1)
            act.activation(sp_[4], sp_[3], ACT.Exp, scale=-1.0).then_inc(r_exp, 1)
            act.wait_ge(r_cum, 1)
            C2 = TILES * HEADS
            act.activation(ecum.rearrange("p r h -> p (r h)"), bank[3][:, 0:C2], ACT.Exp).then_inc(r_ecum, 1)
            act.activation(w_end[:, :, :].rearrange("p r h -> p (r h)"), bank[3][:, C2:2 * C2], ACT.Exp)
            for h in range(HEADS):
                t = act.activation(e_tot[DS * h:DS * h + DS, :],
                                   bank[3][DS * h:DS * h + DS, 2 * C2 + h:3 * C2:HEADS], ACT.Exp)
            t.then_inc(r_tot, 1)
            act.wait_ge(r_ecT, 1)
            act.activation(ecT[0:C2, :], bank[2][0:C2, 0:P], ACT.Copy).then_inc(r_ecS, 1)
            act.wait_ge(r_d, 1)
            act.activation(ex_top, tn[2], ACT.Exp).then_inc(r_ex, 1)

            take_over_b(act)

            def scan(g, w):
                i = 2 * g + w
                q, v = i - 1, 1 - w
                if from_(i, 1) and before(i, QUADS + 1):
                    for h in range(HEADS):
                        act.wait_ge(p_D, HEADS * q + h + 1)
                        if from_(i, 2):
                            act.wait_ge(v_mT, HEADS * (q - 1) + h + 1)
                        act.activation(ed[h], bank[4 if h == 0 else 7][:, :], ACT.Exp).then_inc(s_ed, 1)
                if before(i, QUADS):
                    for s in range(CT):
                        act.wait_ge(p_pre, CT * i + s + 1)
                        if from_(i, 1):
                            act.wait_ge(v_halo, i)
                        act.activation(pre[w][:, s, :, HALO:],
                                       bank[s % 2][:, :].rearrange("p (b t) -> p b t", b=BATCH),
                                       ACT.Copy).then_inc(s_pre, 1)
                    for h in range(HEADS):
                        act.wait_ge(p_z, HEADS * i + h + 1)
                        if from_(i, 2):
                            act.wait_ge(v_yg, HEADS * (i - 1))
                        act.activation(zs[w][:, h, :], bank[1 - h][:, :], ACT.Silu).then_inc(s_z, 1)
                    for s in range(CT):
                        act.wait_ge(v_conv, CT * i + s + 1)
                        if from_(i, 2):
                            act.wait_ge(p_T, CT * (i - 1))
                            act.wait_ge(p_G, i - 1)
                            act.wait_ge(v_yg, HEADS * (i - 1))
                            act.wait_ge(v_ce, i - 1)
                        act.activation(xT[w][:, s, :] if s < HEADS else bcT[w], conv[:, s, :], ACT.Silu,
                                       bias=b_conv[:, s:s + 1]).then_inc(s_xs, 1)
                if from_(i, 1) and before(i, QUADS + 1):
                    for h in range(HEADS):
                        act.wait_ge(v_yg, HEADS * q + h + 1)
                        if from_(i, 2):
                            act.wait_ge(p_O, q)
                        act.activation(sq[:, h, :], yg[:, h, :], ACT.Square).then_inc(s_sq, 1)

            rolled(act, QUADS + 1, 2, 1, 2, scan)

            def evac_rows(i, w):
                v = w % 2
                act.wait_ge(m_T, i + 1)
                if from_(i, 2):
                    act.wait_ge(m_h2, i - 1)
                act.activation(xg[v], bank[4 + v][:, 0:P], ACT.Copy).then_inc(m_xg, 1)

            act.wait_ge(v_out, QUADS)
            act.wait_ge(p_O, QUADS)
            evac_rows(0, 0)

            def moe(g, w):
                j = R8 * g + w
                v = w % 2
                if before(j, BLOCKS):
                    act.wait_ge(m_h1, j + 1)
                    if from_(j, 2):
                        act.wait_ge(m_a, j - 1)
                    act.activation(s1[v][:, 0:HID], bank[v][:, 0:HID], ACT.Silu).then_inc(m_s, 1)
                if from_(j, 2):
                    o = (w - 2) % R8
                    act.wait_ge(m_o, j - 1)
                    if from_(j, R8 + 2):
                        act.wait_ge(m_out[o], 16 * (g if w >= 2 else g - 1))
                    act.activation(yo[o], bank[7][:, 0:D], ACT.Copy).then_inc(m_yo, 1)
                if before(j + 1, BLOCKS):
                    evac_rows(j + 1, w + 1)

            rolled(act, BLOCKS + 2, R8 + 2, 3, R8, moe)

        @block.vector
        def _(ve_):
            link_n = [0]

            def link(ins):
                link_n[0] += 1
                ins.then_inc(v_link, 1)
                ve_.wait_ge(v_link, link_n[0])

            ve_.memset(fill.rearrange("p q r -> p (q r)"), 0.0).then_inc(f_set, 1)
            ve_.wait_ge(f_set, 1)
            ve_.memset(fill[:, :, D + 1].bitcast(U32), OOB).then_inc(f_meta, 1)
            ve_.memset(w3[:, :], 0.0).then_inc(w3_zero, 1)
            for b in range(BATCH):
                s = ve_.memset(state[b][0][:, :], 0.0)
            s.then_inc(s_zero, 1)

            def ln(g, w):
                i = 2 * g + w
                if before(i, QUADS):
                    ve_.wait_ge(x_in[w], 16 * BATCH * (g + 1))
                    for m in range(Q):
                        s = ve_.bn_stats(stats[w][:, m, :], acc[:, Q * i + m, :])
                    s.then_inc(a_stats, 1)
                if from_(i, 2):
                    ve_.wait_ge(a_norm, i - 1)
                    ve_.wait_ge(c_done, 11 + TOP_K * BATCH)
                    for s in range(TOP_K):
                        ve_.tensor_copy(quad(rows[:, s], i - 2)[:, :, 0:D], xn[w]).then_inc(a_row, 1)
                    ve_.wait_ge(a_tr, i - 1)
                    if from_(i, 4):
                        ve_.wait_ge(a_lg, i - 3)
                    ve_.wait_ge(a_cpT, i - 1)
                    if before(i, QUADS):
                        ve_.wait_ge(a_nb, i - 1)
                        ve_.wait_ge(a_stats, i + 1)
                    ve_.tensor_copy(xnTs[w], bank[w][:, :]).then_inc(a_cpTs, 1)
                else:
                    ve_.wait_ge(a_stats, i + 1)
                if before(i, QUADS):
                    for m in range(Q):
                        s = ve_.bn_aggr(mean_var[w][:, m, :], stats[w][:, m, :])
                    s.then_inc(a_mv, 1)

            rolled(ve_, QUADS + 2, 4, 2, 2, ln)

            def wide(t, n, width):
                return t.unsqueeze(2).to_broadcast([P, n, width])

            def mid(t, n, width):
                return t.unsqueeze(1).to_broadcast([P, n, width])

            ve_.wait_ge(c_done, 11 + TOP_K * BATCH)
            ve_.wait_ge(a_lg, QUADS)
            ve_.tensor_copy(lg.rearrange("p r n -> p (r n)"), bank[2][:, 0:TILES * NL]).then_inc(r_lg, 1)
            ve_.wait_ge(r_lg, 1)
            logits = lg[:, :, 0:E]
            for s in range(TOP_K):
                src = logits if s == 0 else V[3]
                link(ve_.tensor_reduce(tn[s], src, AX.X, ALU.max))
                link(ve_.tensor_tensor(V[0], src, wide(tn[s], TILES, E), ALU.is_equal))
                link(ve_.tensor_tensor(V[1], V[0], rank_e[:, :, :], ALU.mult))
                link(ve_.tensor_reduce(tn[3], V[1], AX.X, ALU.max))
                link(ve_.tensor_tensor(hot[s], rank_e[:, :, :], wide(tn[3], TILES, E), ALU.is_equal))
                if s == 0:
                    link(ve_.scalar_tensor_tensor(out=V[3], in0=hot[0], scalar=-3.0e38, in1=logits,
                                                  op0=ALU.mult, op1=ALU.add))
            ve_.tensor_tensor(tn[2], tn[1], tn[0], ALU.subtract).then_inc(r_d, 1)
            ve_.tensor_tensor(VT[0], hot[0].rearrange("p r e -> p e r"), hot[1].rearrange("p r e -> p e r"),
                              ALU.add).then_inc(r_mask, 1)
            ve_.wait_ge(r_ex, 1)
            link(ve_.tensor_scalar(tn[4], ex_top, 1.0, None, ALU.add))
            link(ve_.reciprocal(tn[5], tn[4]))
            ve_.tensor_copy(rows[:, 0, :, D], tn[5])
            link(ve_.tensor_tensor(rows[:, 1, :, D], ex_top, tn[5], ALU.mult))
            ve_.wait_ge(r_cnt, 1)
            flat = "p e r -> p (e r)"
            link(ve_.tensor_copy(VT[1].rearrange(flat), bank[6][:, 0:E * TILES]))
            link(ve_.tensor_tensor_scan(VT[2].rearrange(flat), VT[1].rearrange(flat), VT[1].rearrange(flat), 0.0,
                                        ALU.add, ALU.bypass))
            last = VT[2][:, :, TILES - 1]
            link(ve_.tensor_copy(en[0], last))
            link(ve_.memset(en[1], 0.0))
            link(ve_.tensor_copy(en[1][:, 1:E], last[:, 0:E - 1]))
            link(ve_.tensor_tensor(en[2], en[0], en[1], ALU.subtract))
            link(ve_.tensor_tensor(VT[3], wide(en[2], E, TILES), mid(block_edge[:, :], E, TILES), ALU.is_gt))
            link(ve_.tensor_reduce(en[3], VT[3], AX.X, ALU.add))
            link(ve_.tensor_tensor_scan(en[4], en[3], en[3], 0.0, ALU.add, ALU.bypass))
            link(ve_.tensor_tensor(en[5], en[4], en[3], ALU.subtract))
            link(ve_.scalar_tensor_tensor(out=en[5], in0=en[5], scalar=float(P), in1=en[1],
                                          op0=ALU.mult, op1=ALU.subtract))
            link(ve_.tensor_tensor(VT[2], VT[2], VT[1], ALU.subtract))
            link(ve_.tensor_tensor(VT[2], VT[2], wide(en[5], E, TILES), ALU.add))
            link(ve_.tensor_tensor(VT[2].rearrange(flat), VT[2].rearrange(flat), bank[5][:, 0:E * TILES], ALU.add))
            for s in range(TOP_K):
                link(ve_.tensor_tensor(V[s], hot[s], VT[2].rearrange("p e r -> p r e"), ALU.mult))
                link(ve_.tensor_reduce(tn[s], V[s], AX.X, ALU.add))
                d = ve_.tensor_copy(dest[:, s, :], tn[s])
            d.then_inc(r_dest, 1)
            link(ve_.tensor_tensor(be[0:1], block_no[:, :].unsqueeze(2).to_broadcast([1, BLOCKS, E]),
                                   en[4][0:1].unsqueeze(1).to_broadcast([1, BLOCKS, E]), ALU.is_ge))
            link(ve_.tensor_reduce(bn[0:1], be[0:1], AX.X, ALU.add))
            link(ve_.tensor_scalar(bn[0:1], bn[0:1], float(E - 1), None, ALU.min))
            ve_.tensor_scalar(expert_off[:, 0, :], bn[0:1], float(2 * HID), None, ALU.mult)
            ve_.tensor_scalar(expert_off[:, 1, :], bn[0:1], float(HC * D), None, ALU.mult).then_inc(r_off, 1)

            ve_.wait_ge(wts, 128)
            for h in range(HEADS):
                link(ve_.tensor_scalar(w_out[:, h, :], w_out[:, h, :], w_norm[:, h:h + 1], None, ALU.mult))
            ve_.wait_ge(r_tot, 1)
            take_over_b(ve_)

            for w in range(2):
                h0 = ve_.memset(pre[w][:, :, :, 0:HALO].rearrange("p s b t -> p (s b) t"), 0.0)
            h0.then_inc(v_halo, 1)

            def make_aU(i):
                for h in range(HEADS):
                    if from_(i, 1):
                        ve_.wait_ge(p_D, HEADS * i)
                    ve_.tensor_tensor(aU[:, h, :].rearrange("p (m t) -> p m t", m=Q), mid(upper[:, :], Q, P),
                                      quad(a_all, i)[:, :, h].unsqueeze(2).to_broadcast([P, Q, P]),
                                      ALU.mult).then_inc(v_aU, 1)

            def scan(g, w):
                i = 2 * g + w
                q, v = i - 1, 1 - w
                has_q = from_(i, 1) and before(i, QUADS + 1)
                has_o = from_(i, 2)
                if has_q:
                    for h in range(HEADS):
                        ve_.wait_ge(p_T, CT * q + h + 1)
                        if from_(i, 3):
                            ve_.wait_ge(p_y, KC * (q - 1))
                        ve_.tensor_tensor(xdt[v][:, :, h, :], bank[2 + h][:, :].rearrange("p (m t) -> p m t", m=Q),
                                          quad(dt_all, q)[:, :, h].unsqueeze(2).to_broadcast([P, Q, P]),
                                          ALU.mult).then_inc(v_xdt, 1)
                    ve_.wait_ge(p_T, CT * q + 3)
                    if from_(i, 2):
                        ve_.wait_ge(p_st, q)
                    for h in range(HEADS):
                        b_ = ve_.tensor_tensor(bw[:, :, h, :], bank[2][:, :].rearrange("p (m n) -> p m n", m=Q)[:, :, 0:DS],
                                               quad(w_end, q)[:, :, h].unsqueeze(2).to_broadcast([P, Q, DS]), ALU.mult)
                    b_.then_inc(v_bw, 1)
                    ve_.wait_ge(p_G, q + 1)
                    ve_.tensor_tensor(gT.rearrange("p (m t) -> p m t", m=Q),
                                      bank[3][:, :].rearrange("p (m t) -> p m t", m=Q),
                                      mid(upper[:, :], Q, P), ALU.mult).then_inc(v_gT, 1)
                    ve_.wait_ge(v_gT, q + 1)
                    for h in range(HEADS):
                        ve_.wait_ge(s_ed, HEADS * q + h + 1)
                        if from_(i, 2):
                            ve_.wait_ge(p_y, KC * q)
                        ve_.tensor_tensor(mT[h], ed[h], gT, ALU.mult).then_inc(v_mT, 1)
                    ve_.wait_ge(c_in[v], 16 * HEADS * (g + w))
                    ve_.wait_ge(e_in[v], 16 * HEADS * (g + w))
                    ve_.tensor_tensor(ce, cd[v], ebc[v].rearrange("p m t -> p (m t)"), ALU.mult).then_inc(v_ce, 1)

                def state_step(k):
                    if k == 0:
                        ve_.wait_ge(p_st, q + 1)
                        if from_(i, 2):
                            ve_.wait_ge(p_y, KC * q)
                            ve_.wait_ge(v_S, KC * q)
                        else:
                            ve_.wait_ge(s_zero, 1)
                    else:
                        ve_.wait_ge(p_y, KC * q + 1)
                        ve_.wait_ge(v_S, KC * q + 1)
                    for b in range(BATCH):
                        m = KC * b + k
                        s = ve_.scalar_tensor_tensor(
                            out=state[b][1 - k][:, :], in0=state[b][k][:, :],
                            scalar=e_tot[:, bass.ds(Q * q + m, 1)], in1=bank[7][:, P * m:P * m + P],
                            op0=ALU.mult, op1=ALU.add)
                    s.then_inc(v_S, 1)

                if has_q:
                    state_step(0)
                if has_o:
                    ve_.wait_ge(p_O, i - 1)
                    if from_(i, 4):
                        ve_.wait_ge(g_rms, i - 3)
                    ve_.tensor_scalar(ms[w], bank[1][:, 0:Q], 1.0 / DI, RMS_EPS, ALU.mult, ALU.add).then_inc(v_ms, 1)
                if before(i, QUADS):
                    if from_(i, 1):
                        ve_.wait_ge(s_pre, CT * i)
                        ve_.tensor_copy(pre[w][:, :, :, 0:HALO].rearrange("p s b t -> p (s b) t"),
                                        pre[v][:, :, :, SL_:SL_ + HALO].rearrange("p s b t -> p (s b) t")
                                        ).then_inc(v_halo, 1)
                    ve_.wait_ge(v_halo, i + 1)
                    for k in range(TAPS):
                        for s in range(CT):
                            o = conv[:, s, :].rearrange("p (b t) -> p b t", b=BATCH)
                            x = pre[w][:, s, :, k:k + SL_]
                            if k == 0:
                                ve_.wait_ge(s_pre, CT * i + s + 1)
                                if from_(i, 1):
                                    ve_.wait_ge(s_xs, CT * (i - 1) + s + 1)
                                c = ve_.tensor_scalar(o, x, w_conv[:, s, 0:1], None, ALU.mult)
                            else:
                                ve_.wait_ge(v_tap, (TAPS - 1) * CT * i + (k - 1) * CT + s + 1)
                                c = ve_.scalar_tensor_tensor(out=o, in0=x, scalar=w_conv[:, s, k:k + 1], in1=o,
                                                             op0=ALU.mult, op1=ALU.add)
                            c.then_inc(v_tap if k < TAPS - 1 else v_conv, 1)
                if has_q:
                    state_step(1)
                if has_o:
                    ve_.wait_ge(g_rms, i - 1)
                    for m in range(Q):
                        a = acc[:, Q * (i - 2) + m, :]
                        o = ve_.scalar_tensor_tensor(out=a, in0=bank[4][:, P * m:P * m + P],
                                                     scalar=rms[w][:, m:m + 1], in1=a, op0=ALU.mult, op1=ALU.add)
                    o.then_inc(v_out, 1)
                if has_q:
                    for h in range(HEADS):
                        ve_.wait_ge(p_y, KC * (q + 1))
                        if from_(i, 2):
                            ve_.wait_ge(p_O, q)
                            ve_.wait_ge(s_sq, HEADS * q)
                        ve_.scalar_tensor_tensor(out=yg[:, h, :], in0=xT[v][:, h, :], scalar=d_skip[:, h:h + 1],
                                                 in1=bank[5 + h][:, :], op0=ALU.mult, op1=ALU.add).then_inc(v_ye, 1)
                    for h in range(HEADS):
                        ve_.wait_ge(v_ye, HEADS * q + h + 1)
                        ve_.wait_ge(s_z, HEADS * q + h + 1)
                        ve_.tensor_tensor(yg[:, h, :], yg[:, h, :], zs[v][:, h, :], ALU.mult).then_inc(v_yg, 1)
                if before(i, QUADS):
                    make_aU(i)

            rolled(ve_, QUADS + 2, 4, 2, 2, scan)

            ve_.wait_ge(p_O, QUADS)
            for v in range(2):
                z = ve_.memset(am[v][:, HID:], 0.0)
            z.then_inc(m_pad, 1)

            def moe(g, w):
                j = R8 * g + w
                v = w % 2
                if from_(j, 1) and before(j, BLOCKS + 1):
                    ve_.wait_ge(m_ta, j)
                    if from_(j, 3):
                        ve_.wait_ge(m_o, j - 2)
                    ve_.tensor_copy(amT[1 - v], bank[6][:, 0:HC * P]).then_inc(m_aT, 1)
                if before(j, BLOCKS):
                    ve_.wait_ge(m_h2, j + 1)
                    ve_.wait_ge(m_s, j + 1)
                    if from_(j, 2):
                        ve_.wait_ge(m_ta, j - 1)
                    ve_.scalar_tensor_tensor(out=am[v][:, 0:HID], in0=bank[2 + v][:, 0:HID],
                                             scalar=xin[w][:, D:D + 1], in1=s1[v][:, 0:HID],
                                             op0=ALU.mult, op1=ALU.mult).then_inc(m_a, 1)

            rolled(ve_, BLOCKS + 1, 3, 1, R8, moe)

            ve_.wait_ge(m_yo, BLOCKS)
            for w in range(R8):
                ve_.wait_ge(m_out[w], 16 * (BLOCKS // R8))

            def combine(g, w):
                i = 2 * g + w
                ve_.wait_ge(y_in[w], 16 * BATCH * (g + 1))
                if from_(i, 2):
                    ve_.wait_ge(o_out[w], 16 * BATCH * g)
                ve_.tensor_tensor(res[w], ys[w][:, :, 0, :], ys[w][:, :, 1, :], ALU.add).then_inc(f_sum, 1)
                ve_.wait_ge(f_sum, i + 1)
                ve_.tensor_tensor(res[w], res[w], quad(acc, i), ALU.add).then_inc(f_res, 1)

            rolled(ve_, QUADS, 2, 0, 2, combine)

        @block.tensor
        def _(pe):
            pe.wait_ge(c_done, 11 + TOP_K * BATCH)

            def ln(g, w):
                i = 2 * g + w
                if from_(i, 2):
                    if fixed(i) and i == 2:
                        pe.wait_ge(wts_route, 16 * 2)
                    pe.wait_ge(a_cpTs, i - 1)
                    for m in range(Q):
                        t = pe.matmul(bank[2][:, bass.ds(NL * (Q * (i - 2) + m), NL)], xnTs[w][:, P * m:P * m + P],
                                      w_small[:, :], start=True, stop=True)
                    t.then_inc(a_lg, 1)
                if before(i, QUADS):
                    pe.wait_ge(a_norm, i + 1)
                    if from_(i, 2):
                        pe.wait_ge(a_cpT, i - 1)
                    for m in range(Q):
                        t = pe.transpose(bank[w][:, P * m:P * m + P], xn[w][:, m, :], ident[:, :])
                    t.then_inc(a_tr, 1)

            rolled(pe, QUADS + 2, 4, 2, 2, ln)
            pe.wait_ge(wts, 128)
            pe.wait_ge(r_a, 1)
            C2 = TILES * HEADS
            a2 = a_all[:, :, :].rearrange("p r h -> p (r h)")
            for k, t in enumerate((upper, after, ones)):
                s = pe.matmul(bank[3][:, C2 * k:C2 * k + C2], t[:, :], a2, start=True, stop=True)
            s.then_inc(r_cum, 1)
            pe.wait_ge(r_ecum, 1)
            pe.transpose(bank[2][0:C2, 0:P], ecum.rearrange("p r h -> p (r h)"), ident[:, :]).then_inc(r_ecT, 1)
            pe.wait_ge(r_mask, 1)
            mask = VT[0].rearrange("p e r -> p (e r)")
            pe.matmul(bank[5][:, 0:E * TILES], earlier[:, :], mask, start=True, stop=True)
            pe.matmul(bank[6][:, 0:E * TILES], ones[:, :], mask, start=True, stop=True).then_inc(r_cnt, 1)
            pe.wait_ge(r_tot, 1)
            pe.wait_ge(r_ecS, 1)
            pe.wait_ge(r_dest, 1)

            def scan(g, w):
                i = 2 * g + w
                q, v = i - 1, 1 - w
                has_q = from_(i, 1) and before(i, QUADS + 1)
                if has_q:
                    for h in range(HEADS):
                        pe.wait_ge(v_aU, HEADS * q + h + 1)
                        if from_(i, 3) and h == 0:
                            pe.wait_ge(v_out, q - 1)
                        if from_(i, 2) and h == 1:
                            pe.wait_ge(v_S, KC * q)
                        pe.matmul(bank[4 if h == 0 else 7][:, :], after[:, :], aU[:, h, :],
                                  start=True, stop=True).then_inc(p_D, 1)
                if before(i, QUADS):
                    x = xnT[:, bass.ds(W * i, W)]
                    for s in range(CT):
                        if s == 0 and from_(i, 1):
                            pe.wait_ge(s_z, HEADS * i)
                        if s == 1 and from_(i, 3):
                            pe.wait_ge(v_ms, i - 2)
                        if s == 2:
                            pe.wait_ge(s_pre, CT * i + 1)
                        pe.matmul(bank[s % 2][:, :], w_in[:, DI + P * s:DI + P * s + P], x,
                                  start=True, stop=True).then_inc(p_pre, 1)
                    for h in range(HEADS):
                        pe.wait_ge(s_pre, CT * i + 2 + h)
                        pe.matmul(bank[1 - h][:, :], w_in[:, P * h:P * h + P], x,
                                  start=True, stop=True).then_inc(p_z, 1)
                if has_q:
                    for h in range(HEADS):
                        pe.wait_ge(s_xs, CT * q + h + 1)
                        if from_(i, 2):
                            pe.wait_ge(v_bw if h == 0 else v_gT, q)
                        for m in range(Q):
                            t = pe.transpose(bank[2 + h][:, P * m:P * m + P], xT[v][:, h, P * m:P * m + P], ident[:, :])
                        t.then_inc(p_T, 1)
                    pe.wait_ge(s_xs, CT * q + 3)
                    pe.wait_ge(v_xdt, HEADS * q + 1)
                    for m in range(Q):
                        t = pe.transpose(bank[2][:, P * m:P * m + P], bcT[v][:, P * m:P * m + P], ident[:, :])
                    t.then_inc(p_T, 1)
                    pe.wait_ge(c_in[v], 16 * HEADS * (g + w))
                    pe.wait_ge(v_xdt, HEADS * q + 2)
                    for m in range(Q):
                        t = pe.matmul(bank[3][:, P * m:P * m + P], bcT[v][0:DS, P * m:P * m + P],
                                      cd[v][0:DS, P * m:P * m + P], start=True, stop=True)
                    t.then_inc(p_G, 1)
                if from_(i, 2):
                    r = i - 2
                    pe.wait_ge(v_yg, HEADS * (r + 1))
                    pe.wait_ge(s_sq, HEADS * (r + 1))
                    if before(i, QUADS + 1):
                        pe.wait_ge(s_ed, HEADS * q + 1)
                    if before(i, QUADS):
                        pe.wait_ge(s_z, HEADS * i + 1)
                    for m in range(Q):
                        for h in range(HEADS):
                            pe.matmul(bank[4][:, P * m:P * m + P], yg[:, h, P * m:P * m + P], w_out[:, h, :],
                                      start=(h == 0), stop=(h == HEADS - 1))
                        for h in range(HEADS):
                            t = pe.matmul(bank[1][:, m:m + 1], sq[:, h, P * m:P * m + P], ones[:, 0:1],
                                          start=(h == 0), stop=(h == HEADS - 1))
                    t.then_inc(p_O, 1)
                if has_q:
                    pe.wait_ge(v_xdt, HEADS * (q + 1))
                    pe.wait_ge(v_bw, q + 1)
                    pe.wait_ge(s_ed, HEADS * (q + 1))
                    for m in range(Q):
                        for h in range(HEADS):
                            t = pe.matmul(bank[7][DS * h:DS * h + DS, P * m:P * m + P], bw[:, m, h, :],
                                          xdt[v][:, m, h, :], start=True, stop=True)
                    t.then_inc(p_st, 1)
                    pe.wait_ge(v_mT, HEADS * (q + 1))
                    pe.wait_ge(v_ce, q + 1)
                    if from_(i, 2):
                        pe.wait_ge(v_ye, HEADS * q)
                    else:
                        pe.wait_ge(s_zero, 1)
                    for k in range(KC):
                        if k > 0:
                            pe.wait_ge(v_S, KC * q + k)
                        elif from_(i, 2):
                            pe.wait_ge(v_S, KC * q)
                        for b in range(BATCH):
                            m = KC * b + k
                            for h in range(HEADS):
                                o = bank[5 + h][:, P * m:P * m + P]
                                pe.matmul(o, xdt[v][:, m, h, :], mT[h][:, P * m:P * m + P], start=True, stop=False)
                                t = pe.matmul(o, state[b][k][DS * h:DS * h + DS, :],
                                              ce[DS * h:DS * h + DS, P * m:P * m + P], start=False, stop=True)
                        t.then_inc(p_y, 1)

            rolled(pe, QUADS + 2, 4, 2, 2, scan)

            pe.wait_ge(wts_moe, 16 * (2 + HC))
            pe.wait_ge(r_off, 1)
            pe.wait_ge(v_out, QUADS)
            pe.wait_ge(v_yg, HEADS * QUADS)
            pe.wait_ge(m_pad, 1)

            def turn_rows(g, w):
                j = R8 * g + w
                v = w % 2
                pe.wait_ge(m_in[w], 16 * (g + 1))
                if from_(j, 2):
                    pe.wait_ge(m_xg, j - 1)
                pe.transpose(bank[4 + v][:, 0:P], xin[w][:, 0:D], ident[:, :]).then_inc(m_T, 1)

            turn_rows(0, 0)

            def moe(g, w):
                j = R8 * g + w
                v = w % 2
                if before(j, BLOCKS):
                    off = pe.value_load(expert_off[0:1, 0, bass.ds(j, 1)], min_val=0, max_val=(E - 1) * 2 * HID)
                    pe.wait_ge(m_xg, j + 1)
                    if from_(j, 2):
                        pe.wait_ge(m_s, j - 1)
                    pe.matmul(bank[v][:, 0:HID], xg[v], w12[:, bass.ds(off, HID)], start=True, stop=True
                              ).then_inc(m_h1, 1)
                    if from_(j, 2):
                        pe.wait_ge(m_a, j - 1)
                    pe.matmul(bank[2 + v][:, 0:HID], xg[v], w12[:, bass.ds(off + HID, HID)], start=True, stop=True
                              ).then_inc(m_h2, 1)
                if from_(j, 1) and before(j, BLOCKS + 1):
                    pe.wait_ge(m_a, j)
                    if from_(j, 2):
                        pe.wait_ge(m_aT, j - 1)
                    for k in range(HC):
                        t = pe.transpose(bank[6][:, P * k:P * k + P], am[1 - v][:, P * k:P * k + P], ident[:, :])
                    t.then_inc(m_ta, 1)
                if from_(j, 2):
                    off3 = pe.value_load(expert_off[0:1, 1, bass.ds(j - 2, 1)], min_val=0, max_val=(E - 1) * HC * D)
                    pe.wait_ge(m_aT, j - 1)
                    if from_(j, 3):
                        pe.wait_ge(m_yo, j - 2)
                    for k in range(HC):
                        t = pe.matmul(bank[7][:, 0:D], amT[v][:, P * k:P * k + P],
                                      w3[:, bass.ds(off3 + D * k, D)], start=(k == 0), stop=(k == HC - 1))
                    t.then_inc(m_o, 1)
                if before(j + 1, BLOCKS):
                    turn_rows(g if w < R8 - 1 else g + 1, (w + 1) % R8)

            rolled(pe, BLOCKS + 2, 3, 3, R8, moe)


def kernel(**inputs):
    import numpy as np
    import concourse.bacc as bacc
    from concourse.bass_utils import run_bass_kernel_spmd

    a = {k: np.asarray(v) for k, v in inputs.items()}
    conv_w = a["L0_attn_conv_w"]
    laid = {
        "u": a["L0_attn_u"],
        "in_projT": a["L0_attn_in_proj_w"].T,
        "conv_w": conv_w.reshape(-1, 128, conv_w.shape[2]).transpose(1, 0, 2),
        "conv_b": a["L0_attn_conv_b"].reshape(-1, 128).T,
        "dt_bias": a["L0_attn_dt_bias"],
        "A_log": a["L0_attn_A_log"],
        "D_param": a["L0_attn_D_param"],
        "norm_w": a["L0_attn_norm_w"].reshape(-1, 128).T,
        "out_projT": a["L0_attn_out_proj_w"].T,
        "gateT": a["L0_ffn_gate_w"].T,
        "w1T": a["L0_ffn_w1"].transpose(2, 0, 1),
        "w2T": a["L0_ffn_w2"].transpose(2, 0, 1),
        "w3T": a["L0_ffn_w3"].transpose(2, 0, 1),
    }
    nc = bacc.Bacc("TRN2", target_bir_lowering=False, num_devices=1)
    arrays, args = {}, []
    for name, x in laid.items():
        x = np.ascontiguousarray(x)
        arrays["in_" + name] = x
        args.append(nc.dram_tensor("in_" + name, x.shape, mybir.dt.from_np(x.dtype), kind="ExternalInput").ap())
    out = nc.dram_tensor("out_0", laid["u"].shape, F32, kind="ExternalOutput").ap()
    build(nc, *args, out)
    r = run_bass_kernel_spmd(nc, [arrays], core_ids=[0])
    return r.results[0]["out_0"]
```

```python
from contextlib import ExitStack

import concourse.bass as bass
from concourse import mybir

F32 = mybir.dt.float32
U32 = mybir.dt.uint32
I32 = mybir.dt.int32
ALU = mybir.AluOpType
ACT = mybir.ActivationFunctionType
AX = mybir.AxisListType

P = 128
LN_EPS = 1e-5
RMS_EPS = 1e-5
DECAY_FLOOR = -104.0
TOP_K = 2
OOB = 65535


def rolled(eng, n, head, tail, unroll, body, done=0):
    first = -(-head // unroll)
    last = (n - tail) // unroll
    for s in range(done, first * unroll):
        body(s // unroll, s % unroll)
    with eng.Fori(first, last, 1) as g:
        for u in range(unroll):
            body(g, u)
    for s in range(last * unroll, n):
        body(s // unroll, s % unroll)


def fixed(i):
    return isinstance(i, int)


def from_(i, k):
    return not fixed(i) or i >= k


def before(i, n):
    return not fixed(i) or i < n


def build(nc, u, in_projT, conv_w, conv_b, dt_bias, A_log, D_param, norm_w, out_projT, gateT, w1T, w2T, w3T, out):
    BATCH, SEQ, D = u.shape
    N = BATCH * SEQ
    TILES = N // P
    Q = 4
    KC = Q // BATCH
    QUADS = TILES // Q
    E, HID = w1T.shape[1], w1T.shape[2]
    DI = norm_w.shape[0] * norm_w.shape[1]
    HEADS = dt_bias.shape[0]
    CONV = conv_b.shape[0] * conv_b.shape[1]
    TAPS = conv_w.shape[2]
    DS = (CONV - DI) // 2
    CT = CONV // P
    HALO = TAPS - 1
    W = Q * P
    SL_ = KC * P
    NL = E + HEADS
    HC = -(-HID // P)
    BLOCKS = (N * TOP_K + E * (P - 1)) // P
    ROW = D + 2
    XD = 4
    LAG = 3
    PE_LAG = 2
    R8 = 8
    FILL = 8
    LIST = -(-BLOCKS // FILL) * FILL
    assert D == P and HEADS == 2 and DI == HEADS * P and DS == 64 and CT == 3

    with ExitStack() as ctx:
        def sb(name, shape, dt=F32):
            return ctx.enter_context(nc.sbuf_tensor(name, shape, dt))

        def sem(name):
            return ctx.enter_context(nc.semaphore(name))

        def sems(name, n):
            return [sem(f"{name}{k}") for k in range(n)]

        sorted_rows = nc.dram_tensor("sorted_rows", [LIST * P, ROW], F32, kind="Internal").ap()
        slot_rows = nc.dram_tensor("slot_rows", [N * TOP_K, D], F32, kind="Internal").ap()
        ecum_rows = nc.dram_tensor("ecum_rows", [TILES * HEADS, P], F32, kind="Internal").ap()

        ident = sb("ident", [P, P])
        upper = sb("upper", [P, P])
        after = sb("after", [P, P])
        earlier = sb("earlier", [P, P])
        ones = sb("ones", [P, P])
        neg_half = sb("neg_half", [P, Q])
        eps_c = sb("eps_c", [P, Q])
        minus_c = sb("minus_c", [P, Q])
        rank_e = sb("rank_e", [P, TILES, E])
        block_edge = sb("block_edge", [P, TILES])
        block_no = sb("block_no", [1, BLOCKS])
        w_in = sb("w_in", [P, 2 * DI + 2 * DS + HEADS])
        w_small = sb("w_small", [P, NL])
        w_conv = sb("w_conv", [P, CT, TAPS])
        b_conv = sb("b_conv", [P, CT])
        b_dt = sb("b_dt", [P, HEADS])
        neg_a = sb("neg_a", [P, HEADS])
        a_log = sb("a_log", [P, HEADS])
        d_skip = sb("d_skip", [P, HEADS])
        w_norm = sb("w_norm", [P, HEADS])
        w_out = sb("w_out", [P, HEADS, D])
        HP = HC * P
        EW = 2 * HID + HC * D
        w_exp = sb("w_exp", [P, E * EW])
        w_exp_v = w_exp[:, :].rearrange("p (e n) -> p e n", e=E)

        acc = sb("acc", [P, TILES, D])
        xnT = sb("xnT", [P, TILES * P])
        mamba_out = xnT[:, :].rearrange("p (r d) -> p r d", d=D)
        rows = sb("rows", [P, TOP_K, TILES, ROW])
        dest = sb("dest", [P, TOP_K, TILES], U32)
        dt_all = sb("dt_all", [P, TILES, HEADS])
        a_all = sb("a_all", [P, TILES, HEADS])
        w_end = sb("w_end", [P, TILES, HEADS])
        e_tot = sb("e_tot", [P, TILES])
        expert_off = sb("expert_off", [1, 1 + BLOCKS], I32)
        state = [[sb(f"state{b}{k}", [P, P]) for k in range(2)] for b in range(BATCH)]

        WORK = 24 * 1024
        work = sb("work", [P, WORK])
        used = [0]

        def carve(shape, dt=F32):
            n = 1
            for s in shape:
                n *= s
            a = work[:, used[0]:used[0] + n]
            used[0] += n
            assert used[0] <= WORK, used[0]
            if dt is not F32:
                a = a.bitcast(dt)
            if len(shape) == 1:
                return a
            names = "abcd"[:len(shape)]
            return a.rearrange(f"p ({' '.join(names)}) -> p {' '.join(names)}",
                               **{names[k]: shape[k] for k in range(1, len(shape))})

        pre = [carve([CT, BATCH, HALO + SL_]) for _ in range(2)]
        conv = carve([CT, W])
        early = used[0]
        xT = [carve([HEADS, W]) for _ in range(2)]
        bcT = [carve([W]) for _ in range(2)]
        zs = [carve([HEADS, W]) for _ in range(2)]
        late = used[0]
        xdt = [carve([Q, HEADS, P]) for _ in range(2)]
        ed = [carve([W]) for _ in range(HEADS)]
        cd = [carve([W]) for _ in range(2)]
        ebc = [carve([Q, P]) for _ in range(2)]
        aU = carve([HEADS, W])
        en = [carve([E]) for _ in range(6)]
        be = carve([BLOCKS, E])
        bn = carve([BLOCKS])
        split = used[0]
        used[0] = early
        xn = [carve([Q, D]) for _ in range(XD)]
        xnTs = [carve([W]) for _ in range(XD)]
        stats = [carve([Q, 6]) for _ in range(XD)]
        mean_var = [carve([Q, 2]) for _ in range(XD)]
        ve = [carve([Q]) for _ in range(XD)]
        rstd = [carve([Q]) for _ in range(XD)]
        nmean = [carve([Q]) for _ in range(XD)]
        nbias = [carve([Q]) for _ in range(XD)]
        assert used[0] <= late
        used[0] = split
        fill = carve([FILL, ROW])
        lg = carve([TILES, NL])
        V = [carve([TILES, E]) for _ in range(4)]
        VT = [carve([E, TILES]) for _ in range(5)]
        hot = [carve([TILES, E]) for _ in range(2)]
        tn = [carve([TILES]) for _ in range(6)]
        ex_top = carve([TILES])
        sp_ = [carve([TILES, HEADS]) for _ in range(10)]
        ecum = carve([TILES, HEADS])
        ecT = carve([P])
        used[0] = split
        bw = carve([Q, HEADS, DS])
        gT = carve([W])
        mT = [carve([W]) for _ in range(HEADS)]
        ce = carve([W])
        yg = carve([HEADS, W])
        sq = carve([HEADS, W])
        sq_sum = carve([W])
        ms = [carve([Q]) for _ in range(2)]
        rms = [carve([Q]) for _ in range(2)]
        used[0] = 0
        xin = [carve([ROW]) for _ in range(R8)]
        xg = [carve([P]) for _ in range(2)]
        s1 = [carve([HP]) for _ in range(2)]
        am = [carve([HP]) for _ in range(2)]
        yo = [carve([D]) for _ in range(R8)]
        w12 = [carve([2, HP]) for _ in range(2)]
        ys = [carve([Q, TOP_K, D]) for _ in range(QUADS)]
        res = [carve([Q, D]) for _ in range(QUADS)]

        bank = [ctx.enter_context(nc.psum_tensor(f"bank{k}", [P, 512], F32)) for k in range(8)]

        wts_route = sem("router_weights_in")
        wts = sem("weights_in")
        wts_moe = sem("expert_weights_in")
        c_one = sem("constant_filled")
        c_done = sem("constants_ready")
        f_set = sem("fill_ready")
        f_meta = sem("fill_meta")
        f_out = sem("list_filled")
        s_zero = sem("states_zeroed")
        w3_zero = sem("w3_zeroed")
        x_in = sems("x_in", XD)
        a_stats, a_mv, a_ve, a_rstd, a_nb, a_norm, a_row, a_tr, a_cpT, a_cpTs, a_lg = (
            sem(n) for n in ("ln_stats", "ln_mean_var", "ln_ve", "ln_rstd", "ln_bias", "ln_normed", "ln_rows",
                             "ln_transposed", "xnT_ready", "xnTs_ready", "logits_ready"))
        v_link = sem("vector_step")
        g_link = sem("gpsimd_step")
        r_lg = sem("logits_copied")
        r_d = sem("top_gap_ready")
        r_ex = sem("top_exp_ready")
        r_mask = sem("route_mask_ready")
        r_cnt = sem("route_counts_ready")
        r_dest = sem("destinations_ready")
        r_off = sem("expert_offsets_ready")
        r_abs = sem("dt_abs_ready")
        r_exp = sem("dt_exp_ready")
        r_den = sem("series_divisor_ready")
        r_inv = sem("series_divisor_inverted")
        r_na = sem("exp_a_log_ready")
        r_a = sem("decays_ready")
        r_cum = sem("cumulated_ready")
        r_ecum = sem("ecum_ready")
        r_tot = sem("chunk_decays_ready")
        r_ecT = sem("ecum_transposed")
        r_ecS = sem("ecum_copied")
        r_ecD = sem("ecum_stored")
        r_wo = sem("w_out_ready")
        sc_in = sem("rows_scattered")
        p_pre, p_z, p_T, p_G, p_D, p_st, p_y, p_O = (
            sem(n) for n in ("conv_in_projected", "z_projected", "x_transposed", "bc_product", "decay_sums",
                             "state_added", "y_ready", "out_projected"))
        s_pre, s_z, s_xs, s_ed, s_sq, s_out = (sem(n) for n in ("pre_copied", "z_silued", "conv_silued",
                                                                "decays_exped", "squares_ready", "mamba_ready"))
        v_halo, v_tap, v_conv, v_xdt, v_bw, v_gT, v_mT, v_S, v_ye, v_yg, v_ms = (
            sem(n) for n in ("halo_copied", "tap_added", "conv_ready", "xdt_ready", "bw_ready", "gT_ready",
                             "mT_ready", "state_ready", "y_skip_added", "y_gated", "mean_square_ready"))
        g_sq = sem("squares_summed")
        g_rms, g_ce, g_aU = sem("rms_ready"), sem("ce_ready"), sem("aU_ready")
        e_in = sems("ecum_in", 2)
        c_in = sems("c_copied", 2)
        m_in = sems("block_in", R8)
        m_T, m_h1, m_h2, m_o = (sem(n) for n in ("rows_transposed", "h1_ready", "h2_ready", "expert_out_ready"))
        m_w, m_xg, m_s, m_a, m_yo = (sem(n) for n in ("w1_w2_copied", "rowsT_ready", "silu_ready", "act_ready",
                                                      "expert_rows_ready"))
        m_out = sems("expert_rows_out", R8)
        y_in = sems("slots_in", QUADS)
        f_acc = sem("mamba_added")
        f_sum, f_res = sem("slots_summed"), sem("result_ready")
        o_out = sem("result_out")

        block = ctx.enter_context(nc.Block())

        def tiles_view(dram):
            return dram.rearrange("b (i k p) d -> i p b k d", k=KC, p=P)

        u_v, out_v = tiles_view(u), tiles_view(out)
        slots_v = slot_rows.rearrange("(b i k p s) d -> i p b k (s d)", b=BATCH, k=KC, p=P, s=TOP_K)
        ecum_v = ecum_rows.rearrange("(i m h) t -> i h m t", m=Q, h=HEADS)
        sorted_v = sorted_rows.rearrange("(n p) r -> n p r", p=P)

        DECAY_HEADS = [(1, bank[7]), (0, bank[4])]

        def quad(t, i):
            return t[:, bass.ds(Q * i, Q)]

        def take_over_b(eng):
            eng.wait_ge(a_row, TOP_K * QUADS)
            eng.wait_ge(f_out, 16 * LIST // FILL)
            eng.wait_ge(r_ecD, 16)
            eng.wait_ge(r_dest, 1)

        def results_out(eng):
            for w in range(R8):
                eng.wait_ge(m_out[w], 16 * (-(-(BLOCKS - w) // R8)))

        @block.sync
        def _(sp):
            def load_x(g, w):
                i = XD * g + w
                if from_(i, XD):
                    sp.wait_ge(a_stats, i - XD + 1)
                for b in range(BATCH):
                    sp.dma_start(acc[:, bass.ds(Q * i + KC * b, KC), :],
                                 u_v[i][:, b]).then_inc(x_in[w], 16)
                if fixed(i) and i == 1:
                    sp.dma_start(w_small[:, 0:E], gateT).then_inc(wts_route, 16)
                    sp.dma_start(w_small[:, E:NL], in_projT[:, 2 * DI + 2 * DS:]).then_inc(wts_route, 16)

            def small_weights():
                sp.dma_start(b_dt[:, :], dt_bias.partition_broadcast(P)).then_inc(wts, 16)
                sp.dma_start(a_log[:, :], A_log.partition_broadcast(P)).then_inc(wts, 16)
                sp.dma_start(d_skip[:, :], D_param.partition_broadcast(P)).then_inc(wts, 16)
                sp.dma_start(w_norm[:, :], norm_w).then_inc(wts, 16)
                sp.dma_start(b_conv[:, :], conv_b).then_inc(wts, 16)
                sp.dma_start(w_conv[:, :, :], conv_w).then_inc(wts, 16)
                sp.dma_start(w_out[:, :, :], out_projT.rearrange("(h p) d -> p h d", p=P)).then_inc(wts, 16)
                sp.dma_start(w_in[:, :], in_projT).then_inc(wts, 16)

            rolled(sp, QUADS, XD, 0, XD, load_x)
            small_weights()
            sp.wait_ge(f_set, 1)
            sp.wait_ge(f_meta, 1)
            fv = sorted_rows.rearrange("(p c q) r -> c p (q r)", p=P, q=FILL)
            for c in range(LIST // FILL):
                sp.dma_start(fv[c], fill.rearrange("p q r -> p (q r)")).then_inc(f_out, 16)
            sp.dma_start(w_exp_v[:, :, 0:HID], w1T).then_inc(wts_moe, 16)
            sp.dma_start(w_exp_v[:, :, HID:2 * HID], w2T).then_inc(wts_moe, 16)
            sp.wait_ge(w3_zero, 1)
            for k in range(HC):
                m = min(P, HID - k * P)
                sp.dma_start(w_exp_v[0:m, :, 2 * HID + D * k:2 * HID + D * k + D],
                             w3T[k * P:k * P + m]).then_inc(wts_moe, 16)
            sp.wait_ge(r_ecS, 1)
            sp.dma_start(ecum_rows, ecT[0:TILES * HEADS, :]).then_inc(r_ecD, 16)

            sp.wait_ge(r_ecD, 16)

            def feed(g, w):
                i = 2 * g + w
                if from_(i, 2):
                    sp.wait_ge(g_ce, i - 1)
                src = ecum_v[i]
                for h in range(HEADS):
                    sp.dma_start(ebc[w][DS * h:DS * h + DS],
                                 src[h].partition_broadcast(DS)).then_inc(e_in[w], 16)
                sp.wait_ge(s_xs, 3 * i + 3)
                if from_(i, 2):
                    sp.wait_ge(p_G, i - 1)
                for h in range(HEADS):
                    sp.dma_start(cd[w][DS * h:DS * h + DS, :], bcT[w][DS:2 * DS, :]).then_inc(c_in[w], 16)

            rolled(sp, QUADS, 2, 0, 2, feed)

            sp.wait_ge(sc_in, 16 * TOP_K * TILES)
            sp.wait_ge(v_conv, CT * QUADS)
            sp.wait_ge(s_xs, CT * QUADS)

            def load_block(g, w):
                if from_(g, 1):
                    sp.wait_ge(m_out[w], 16 * g)
                j = R8 * g + w
                sp.dma_start(xin[w], sorted_v[j]).then_inc(m_in[w], 16)

            rolled(sp, BLOCKS, R8, 0, R8, load_block)

            results_out(sp)
            for i in range(QUADS):
                for b in range(BATCH):
                    sp.dma_start(ys[i][:, KC * b:KC * b + KC].rearrange("p k s d -> p k (s d)"),
                                 slots_v[i][:, b]).then_inc(y_in[i], 16)

        @block.gpsimd
        def _(gp):
            def tri(t, pattern, cm, op):
                gp.affine_select(out=t[:, :], in_=t[:, :], compare_op=op, fill=0.0, base=0,
                                 pattern=[[pattern, P]], channel_multiplier=cm).then_inc(c_done, 1)

            gp.memset(ident[:, :], 0.0).then_inc(c_one, 1)
            for t in (upper, after, earlier):
                gp.memset(t[:, :], 1.0).then_inc(c_one, 1)
            gp.wait_ge(c_one, 4)
            gp.affine_select(out=ident[:, :], in_=ident[:, :], compare_op=ALU.not_equal, fill=1.0, base=0,
                             pattern=[[-1, P]], channel_multiplier=1).then_inc(c_done, 1)
            gp.memset(neg_half[:, :], -0.5).then_inc(c_done, 1)
            gp.memset(eps_c[:, :], LN_EPS).then_inc(c_done, 1)
            gp.memset(minus_c[:, :], -1.0).then_inc(c_done, 1)
            tri(upper, 1, -1, ALU.is_ge)
            tri(after, -1, 1, ALU.is_gt)
            tri(earlier, 1, -1, ALU.is_gt)
            gp.memset(ones[:, :], 1.0).then_inc(c_done, 1)

            gp.iota(rank_e[:, :, :], [[0, TILES], [-1, E]], base=E, channel_multiplier=0,
                    allow_small_or_imprecise_dtypes=True).then_inc(c_done, 1)
            gp.iota(block_edge[:, :], [[P, TILES]], base=0, channel_multiplier=0,
                    allow_small_or_imprecise_dtypes=True).then_inc(c_done, 1)
            gp.iota(block_no[:, :], [[1, BLOCKS]], base=0, channel_multiplier=0,
                    allow_small_or_imprecise_dtypes=True).then_inc(c_done, 1)
            for s in range(TOP_K):
                for b in range(BATCH):
                    gp.iota(rows[:, s].bitcast(U32).rearrange("p (i b k) r -> p b i k r", b=BATCH, k=KC)
                            [:, b, :, :, D + 1],
                            [[TOP_K * KC * P, QUADS], [TOP_K * P, KC]], base=TOP_K * SEQ * b + s,
                            channel_multiplier=TOP_K).then_inc(c_done, 1)

            def ln(g, w):
                i = XD * g + w
                gp.wait_ge(a_mv, i + 1)
                if from_(i, XD):
                    gp.wait_ge(a_norm, i - XD + 1)
                gp.tensor_tensor(ve[w], mean_var[w][:, :, 1], eps_c[:, :], ALU.add).then_inc(a_ve, 1)
                gp.tensor_tensor(nmean[w], mean_var[w][:, :, 0], minus_c[:, :], ALU.mult).then_inc(a_ve, 1)
                gp.wait_ge(a_ve, 2 * i + 2)
                gp.tensor_tensor(rstd[w], ve[w], neg_half[:, :], ALU.pow).then_inc(a_rstd, 1)
                gp.wait_ge(a_rstd, i + 1)
                gp.tensor_tensor(nbias[w], nmean[w], rstd[w], ALU.mult).then_inc(a_nb, 1)

            gp.wait_ge(c_done, 11 + TOP_K * BATCH)
            rolled(gp, QUADS, XD, 0, XD, ln)

            steps = [0]

            def link(ins):
                steps[0] += 1
                ins.then_inc(g_link, 1)
                gp.wait_ge(g_link, steps[0])

            def wide2(t):
                return t.unsqueeze(1).to_broadcast([P, TILES, HEADS])

            gp.wait_ge(r_lg, 1)
            gp.wait_ge(wts, 128)
            x, relu, twice, mag, e, den, inv, s_, s2, poly = sp_
            link(gp.tensor_tensor(x, lg[:, :, E:NL], wide2(b_dt[:, :]), ALU.add))
            link(gp.tensor_scalar(relu, x, 0.0, None, ALU.max))
            link(gp.tensor_tensor(twice, relu, relu, ALU.add))
            gp.tensor_tensor(mag, twice, x, ALU.subtract).then_inc(r_abs, 1)
            gp.wait_ge(r_na, 1)
            link(gp.tensor_scalar(neg_a[:, :], neg_a[:, :], -1.0, None, ALU.mult))
            gp.wait_ge(r_exp, 1)
            gp.tensor_scalar(den, e, 2.0, None, ALU.add).then_inc(r_den, 1)
            gp.wait_ge(r_inv, 1)
            link(gp.tensor_tensor(s_, e, inv, ALU.mult))
            link(gp.tensor_tensor(s2, s_, s_, ALU.mult))
            link(gp.tensor_scalar(poly, s2, 1.0 / 15, 1.0 / 13, ALU.mult, ALU.add))
            for c in (11, 9, 7, 5, 3, 1):
                link(gp.tensor_tensor(poly, poly, s2, ALU.mult))
                link(gp.tensor_scalar(poly, poly, 1.0, 1.0 / c, ALU.mult, ALU.add))
            link(gp.tensor_tensor(poly, poly, s_, ALU.mult))
            link(gp.tensor_tensor(poly, poly, poly, ALU.add))
            link(gp.tensor_tensor(dt_all[:, :, :], poly, relu, ALU.add))
            link(gp.tensor_tensor(inv, dt_all[:, :, :], wide2(neg_a[:, :]), ALU.mult))
            gp.tensor_scalar(a_all[:, :, :], inv, DECAY_FLOOR, None, ALU.max).then_inc(r_a, 1)

            def make_aU(i):
                for h, _ in DECAY_HEADS:
                    if i >= 1:
                        gp.wait_ge(p_D, HEADS * i)
                    gp.tensor_tensor(aU[:, h, :].rearrange("p (m t) -> p m t", m=Q),
                                     upper[:, :].unsqueeze(1).to_broadcast([P, Q, P]),
                                     quad(a_all, i)[:, :, h].unsqueeze(2).to_broadcast([P, Q, P]),
                                     ALU.mult).then_inc(g_aU, 1)

            def make_ce(q):
                v = q % 2
                gp.wait_ge(c_in[v], 16 * HEADS * (q // 2 + 1))
                gp.wait_ge(e_in[v], 16 * HEADS * (q // 2 + 1))
                if q >= 1:
                    gp.wait_ge(p_y, KC * q)
                gp.tensor_tensor(ce, cd[v], ebc[v].rearrange("p m t -> p (m t)"), ALU.mult).then_inc(g_ce, 1)

            all_rows = [(s, r) for r in range(TILES) for s in range(TOP_K)]

            def scatter(n):
                for s, r in all_rows[:n]:
                    gp.indirect_dma_start(
                        out=sorted_rows, out_offset=bass.IndirectOffsetOnAxis(ap=dest[:, s, r:r + 1], axis=0),
                        in_=rows[:, s, r, :], in_offset=None).then_inc(sc_in, 16)
                del all_rows[:n]

            gp.wait_ge(r_a, 1)
            make_aU(0)
            make_aU(1)
            for i in range(1, QUADS + 2):
                if i == 1:
                    take_over_b(gp)
                if i >= 2:
                    gp.wait_ge(s_sq, HEADS * (i - 1))
                    if i >= 3:
                        gp.wait_ge(p_O, i - 2)
                    gp.tensor_tensor(sq_sum, sq[:, 0, :], sq[:, 1, :], ALU.add).then_inc(g_sq, 1)
                if 2 <= i < QUADS:
                    make_aU(i)
                if i <= QUADS:
                    make_ce(i - 1)
                scatter(2 if i > 1 else 14)
                if i >= 2:
                    gp.wait_ge(v_ms, i - 1)
                    if i >= 4:
                        gp.wait_ge(s_out, i - 3)
                    gp.tensor_tensor(rms[i % 2], ms[i % 2], neg_half[:, :], ALU.pow).then_inc(g_rms, 1)
                    scatter(6)
            assert not all_rows

            bound = gp.to_reg(N * TOP_K - 1)

            def put(g, w):
                gp.wait_ge(m_yo, R8 * g + w + 1)
                gp.wait_ge(m_in[w], 16 * (g + 1))
                gp.indirect_dma_start(
                    out=slot_rows, out_offset=bass.IndirectOffsetOnAxis(ap=xin[w][:, D + 1:D + 2].bitcast(U32), axis=0),
                    in_=yo[w], in_offset=None, bounds_check=bound, oob_is_err=False).then_inc(m_out[w], 16)

            for j in range(BLOCKS):
                put(j // R8, j % R8)

        @block.scalar
        def _(act):
            def norm(g, w):
                i = XD * g + w
                if from_(i, 2):
                    act.wait_ge(a_tr, i - 1)
                    act.activation(xnT[:, bass.ds(W * (i - 2), W)], bank[(w - 2) % XD][:, :],
                                   ACT.Copy).then_inc(a_cpT, 1)
                if before(i, QUADS):
                    act.wait_ge(a_nb, i + 1)
                    if from_(i, XD):
                        act.wait_ge(a_row, TOP_K * (i - XD + 1))
                    for m in range(Q):
                        n = act.activation(xn[w][:, m, :], acc[:, Q * i + m, :],
                                           ACT.Identity, bias=nbias[w][:, m:m + 1], scale=rstd[w][:, m:m + 1])
                    n.then_inc(a_norm, 1)

            rolled(act, QUADS + 2, XD, 2, XD, norm)

            def evac_pre(g, w, cs):
                i = 2 * g + w
                for c in cs:
                    act.wait_ge(p_pre, CT * i + c + 1)
                    if from_(i, 1):
                        act.wait_ge(v_halo, i)
                        act.wait_ge(s_xs, CT * (i - 1) + c + 1)
                    act.activation(pre[w][:, c, :, HALO:],
                                   bank[c % 2][:, :].rearrange("p (b t) -> p b t", b=BATCH), ACT.Copy)
                    act.activation(conv[:, c, :], bank[c % 2][:, :], ACT.Copy,
                                   scale=w_conv[:, c, TAPS - 1:TAPS]).then_inc(s_pre, 1)

            def silu_z(g, w):
                i = 2 * g + w
                for h in range(HEADS):
                    act.wait_ge(p_z, HEADS * i + h + 1)
                    if from_(i, 2):
                        act.wait_ge(v_yg, HEADS * (i - 1))
                    act.activation(zs[w][:, h, :], bank[1 - h][:, :], ACT.Silu).then_inc(s_z, 1)

            def silu_conv(g, w):
                i = 2 * g + w
                for c in range(CT):
                    act.wait_ge(v_conv, CT * i + c + 1)
                    if from_(i, 2):
                        act.wait_ge(p_T, CT * (i - 1))
                        act.wait_ge(p_G, i - 1)
                        act.wait_ge(v_yg, HEADS * (i - 1))
                        act.wait_ge(g_ce, i - 1)
                    act.activation(xT[w][:, c, :] if c < HEADS else bcT[w], conv[:, c, :], ACT.Silu,
                                   bias=b_conv[:, c:c + 1]).then_inc(s_xs, 1)

            act.wait_ge(wts, 128)
            for h in range(HEADS):
                f_ = act.activation(w_out[:, h, :], w_out[:, h, :], ACT.Copy, scale=w_norm[:, h:h + 1])
            f_.then_inc(r_wo, 1)
            act.activation(neg_a[:, :], a_log[:, :], ACT.Exp).then_inc(r_na, 1)
            act.wait_ge(r_abs, 1)
            act.activation(sp_[4], sp_[3], ACT.Exp, scale=-1.0).then_inc(r_exp, 1)
            evac_pre(0, 0, range(CT))
            act.wait_ge(r_d, 1)
            act.activation(ex_top, tn[2], ACT.Exp).then_inc(r_ex, 1)
            act.wait_ge(r_cum, 1)
            C2 = TILES * HEADS
            act.activation(ecum.rearrange("p r h -> p (r h)"), bank[3][:, 0:C2], ACT.Exp).then_inc(r_ecum, 1)
            act.activation(w_end[:, :, :].rearrange("p r h -> p (r h)"), bank[3][:, C2:2 * C2], ACT.Exp)
            for h in range(HEADS):
                t = act.activation(e_tot[DS * h:DS * h + DS, :],
                                   bank[3][DS * h:DS * h + DS, 2 * C2 + h:3 * C2:HEADS], ACT.Exp)
            t.then_inc(r_tot, 1)
            act.wait_ge(r_ecT, 1)
            act.activation(ecT[0:C2, :], bank[2][0:C2, 0:P], ACT.Copy).then_inc(r_ecS, 1)
            act.wait_ge(a_row, TOP_K * QUADS)
            act.wait_ge(a_lg, QUADS)
            silu_z(0, 0)
            silu_conv(0, 0)

            def mamba(r, w):
                act.wait_ge(p_O, r + 1)
                act.wait_ge(g_rms, r + 1)
                for m in range(Q):
                    o = act.activation(mamba_out[:, Q * r + m, :],
                                       bank[4][:, P * m:P * m + P], ACT.Copy, scale=rms[w][:, m:m + 1])
                o.then_inc(s_out, 1)

            def scan(g, w):
                i = 2 * g + w
                q, r = i - 1, i - 2
                has_q = from_(i, 1) and before(i, QUADS + 1)
                has_i = before(i, QUADS)

                def decays(n):
                    h, src = DECAY_HEADS[n]
                    act.wait_ge(p_D, HEADS * q + n + 1)
                    if from_(i, 2):
                        act.wait_ge(v_mT, HEADS * (q - 1) + n + 1)
                    act.activation(ed[h], src[:, :], ACT.Exp).then_inc(s_ed, 1)

                if from_(i, 3) and before(i, QUADS + 1):
                    mamba(r - 1, 1 - w)
                if has_q:
                    decays(0)
                if has_i:
                    evac_pre(g, w, (0,))
                if has_q:
                    decays(1)
                if has_i:
                    evac_pre(g, w, (1,))
                if from_(i, 2):
                    if fixed(i) and i == 2:
                        take_over_b(act)
                    for h in range(HEADS):
                        act.wait_ge(v_yg, HEADS * r + h + 1)
                        if from_(i, 3):
                            act.wait_ge(g_sq, r)
                        act.activation(sq[:, h, :], yg[:, h, :], ACT.Square).then_inc(s_sq, 1)
                if has_i:
                    evac_pre(g, w, (2,))
                    silu_z(g, w)
                    silu_conv(g, w)

            rolled(act, QUADS + 1, 4, 1, 2, scan, done=1)

            def evac_rows(i, w):
                v = w % 2
                act.wait_ge(m_T, i + 1)
                if from_(i, 2):
                    act.wait_ge(m_h2, i - 1)
                act.activation(xg[v], bank[2][:, 0:P], ACT.Copy).then_inc(m_xg, 1)

            mamba(QUADS - 2, 0)
            evac_rows(0, 0)

            def moe(g, w):
                j = R8 * g + w
                v = w % 2
                if before(j, BLOCKS):
                    act.wait_ge(m_h1, j + 1)
                    if from_(j, 2):
                        act.wait_ge(m_a, j - 1)
                    act.activation(s1[v], bank[v][:, 0:HP], ACT.Silu).then_inc(m_s, 1)
                if before(j + 1, BLOCKS):
                    evac_rows(j + 1, w + 1)
                if from_(j, 1):
                    o = (w - 1) % R8
                    act.wait_ge(m_o, j)
                    if from_(j, R8 + 1):
                        act.wait_ge(m_out[o], 16 * (g if w >= 1 else g - 1))
                    act.activation(yo[o], bank[3][:, 0:D], ACT.Copy, scale=xin[o][:, D:D + 1]).then_inc(m_yo, 1)

            moe(0, 0)
            scan(QUADS // 2, 1)
            moe(0, 1)
            moe(0, 2)
            mamba(QUADS - 1, 1)
            rolled(act, BLOCKS + 1, R8 + 1, 2, R8, moe, done=3)

            for i in range(QUADS):
                act.wait_ge(f_res, i + 1)
                for b in range(BATCH):
                    act.dma_start(out_v[i][:, b], res[i][:, KC * b:KC * b + KC, :]).then_inc(o_out, 16)
            act.wait_ge(o_out, 16 * BATCH * QUADS)

        @block.vector
        def _(ve_):
            link_n = [0]

            def link(ins):
                link_n[0] += 1
                ins.then_inc(v_link, 1)
                ve_.wait_ge(v_link, link_n[0])

            ve_.memset(fill.rearrange("p q r -> p (q r)"), 0.0).then_inc(f_set, 1)
            ve_.wait_ge(f_set, 1)
            ve_.memset(fill[:, :, D + 1].bitcast(U32), OOB).then_inc(f_meta, 1)
            ve_.memset(w_exp_v[(HID % P) // 32 * 32:, :, EW - D:], 0.0).then_inc(w3_zero, 1)
            for b in range(BATCH):
                s = ve_.memset(state[b][0][:, :], 0.0)
            s.then_inc(s_zero, 1)

            def ln(g, w):
                i = XD * g + w
                o = (w - LAG) % XD
                if before(i, QUADS):
                    ve_.wait_ge(x_in[w], 16 * BATCH * (g + 1))
                    for m in range(Q):
                        s = ve_.bn_stats(stats[w][:, m, :], acc[:, Q * i + m, :])
                    s.then_inc(a_stats, 1)

                def copy_rows(s):
                    ve_.tensor_copy(quad(rows[:, s], i - LAG)[:, :, 0:D], xn[o]).then_inc(a_row, 1)

                if from_(i, LAG):
                    ve_.wait_ge(a_norm, i - LAG + 1)
                    ve_.wait_ge(c_done, 11 + TOP_K * BATCH)
                    if before(i, QUADS):
                        if from_(i, XD):
                            ve_.wait_ge(a_nb, i - XD + 1)
                        ve_.wait_ge(a_stats, i + 1)
                    copy_rows(0)
                else:
                    ve_.wait_ge(a_stats, i + 1)
                if before(i, QUADS):
                    for m in range(Q):
                        s = ve_.bn_aggr(mean_var[w][:, m, :], stats[w][:, m, :])
                    s.then_inc(a_mv, 1)
                if from_(i, LAG):
                    copy_rows(1)
                    ve_.wait_ge(a_tr, i - LAG + 1)
                    ve_.wait_ge(a_cpT, i - LAG + 1)
                    ve_.tensor_copy(xnTs[o], bank[o][:, :]).then_inc(a_cpTs, 1)

            rolled(ve_, QUADS + LAG, XD, LAG, XD, ln)

            def wide(t, n, width):
                return t.unsqueeze(2).to_broadcast([P, n, width])

            def mid(t, n, width):
                return t.unsqueeze(1).to_broadcast([P, n, width])

            def halo(g, w):
                i, v = 2 * g + w, 1 - w
                ve_.wait_ge(s_pre, CT * i)
                ve_.tensor_copy(pre[w][:, :, :, 0:HALO].rearrange("p s b t -> p (s b) t"),
                                pre[v][:, :, :, SL_:SL_ + HALO].rearrange("p s b t -> p (s b) t")
                                ).then_inc(v_halo, 1)

            def conv_taps(g, w, cs, between=None):
                i = 2 * g + w
                done = (HALO - 1) * (CT * i + cs[0])
                if cs[0] == 0:
                    ve_.wait_ge(v_halo, i + 1)
                for k in range(HALO):
                    if between and k == 1:
                        between()
                    for n, c in enumerate(cs):
                        o = conv[:, c, :].rearrange("p (b t) -> p b t", b=BATCH)
                        if k == 0:
                            ve_.wait_ge(s_pre, CT * i + c + 1)
                        else:
                            ve_.wait_ge(v_tap, done + len(cs) * (k - 1) + n + 1)
                        ve_.scalar_tensor_tensor(out=o, in0=pre[w][:, c, :, k:k + SL_], scalar=w_conv[:, c, k:k + 1],
                                                 in1=o, op0=ALU.mult, op1=ALU.add
                                                 ).then_inc(v_tap if k < HALO - 1 else v_conv, 1)

            for w in range(2):
                h0 = ve_.memset(pre[w][:, :, :, 0:HALO].rearrange("p s b t -> p (s b) t"), 0.0)
            h0.then_inc(v_halo, 1)
            ve_.wait_ge(c_done, 11 + TOP_K * BATCH)
            ve_.wait_ge(a_lg, QUADS)
            ve_.tensor_copy(lg.rearrange("p r n -> p (r n)"), bank[7][:, 0:TILES * NL]).then_inc(r_lg, 1)
            ve_.wait_ge(r_lg, 1)
            logits = lg[:, :, 0:E]
            for s in range(TOP_K):
                src = logits if s == 0 else V[3]
                link(ve_.tensor_reduce(tn[s], src, AX.X, ALU.max))
                link(ve_.tensor_tensor(V[0], src, wide(tn[s], TILES, E), ALU.is_equal))
                link(ve_.tensor_tensor(V[1], V[0], rank_e[:, :, :], ALU.mult))
                link(ve_.tensor_reduce(tn[3], V[1], AX.X, ALU.max))
                link(ve_.tensor_tensor(hot[s], rank_e[:, :, :], wide(tn[3], TILES, E), ALU.is_equal))
                if s == 0:
                    link(ve_.scalar_tensor_tensor(out=V[3], in0=hot[0], scalar=-3.0e38, in1=logits,
                                                  op0=ALU.mult, op1=ALU.add))
                    ve_.wait_ge(r_den, 1)
                    ve_.reciprocal(sp_[6], sp_[5]).then_inc(r_inv, 1)
            ve_.tensor_tensor(tn[2], tn[1], tn[0], ALU.subtract).then_inc(r_d, 1)
            ve_.tensor_tensor(VT[0], hot[0].rearrange("p r e -> p e r"), hot[1].rearrange("p r e -> p e r"),
                              ALU.add).then_inc(r_mask, 1)
            ve_.wait_ge(wts, 128)
            conv_taps(0, 0, range(CT))
            ve_.wait_ge(r_ex, 1)
            link(ve_.tensor_scalar(tn[4], ex_top, 1.0, None, ALU.add))
            link(ve_.reciprocal(tn[5], tn[4]))
            ve_.tensor_copy(rows[:, 0, :, D], tn[5])
            link(ve_.tensor_tensor(rows[:, 1, :, D], ex_top, tn[5], ALU.mult))
            ve_.wait_ge(r_cnt, 1)
            flat = "p e r -> p (e r)"
            link(ve_.tensor_copy(VT[1].rearrange(flat), bank[6][:, 0:E * TILES]))
            link(ve_.tensor_tensor_scan(VT[2].rearrange(flat), VT[1].rearrange(flat), VT[1].rearrange(flat), 0.0,
                                        ALU.add, ALU.bypass))
            last = VT[2][:, :, TILES - 1]
            link(ve_.tensor_copy(en[0], last))
            link(ve_.memset(en[1], 0.0))
            link(ve_.tensor_copy(en[1][:, 1:E], last[:, 0:E - 1]))
            link(ve_.tensor_tensor(en[2], en[0], en[1], ALU.subtract))
            link(ve_.tensor_tensor(VT[3], wide(en[2], E, TILES), mid(block_edge[:, :], E, TILES), ALU.is_gt))
            link(ve_.tensor_reduce(en[3], VT[3], AX.X, ALU.add))
            link(ve_.tensor_tensor_scan(en[4], en[3], en[3], 0.0, ALU.add, ALU.bypass))
            link(ve_.tensor_tensor(en[5], en[4], en[3], ALU.subtract))
            link(ve_.scalar_tensor_tensor(out=en[5], in0=en[5], scalar=float(P), in1=en[1],
                                          op0=ALU.mult, op1=ALU.subtract))
            link(ve_.tensor_tensor(VT[2], VT[2], VT[1], ALU.subtract))
            link(ve_.tensor_tensor(VT[2], VT[2], wide(en[5], E, TILES), ALU.add))
            link(ve_.tensor_tensor(VT[2].rearrange(flat), VT[2].rearrange(flat), bank[5][:, 0:E * TILES], ALU.add))
            for s in range(TOP_K):
                link(ve_.tensor_tensor(V[s], hot[s], VT[2].rearrange("p e r -> p r e"), ALU.mult))
                link(ve_.tensor_reduce(tn[s], V[s], AX.X, ALU.add))
                d = ve_.tensor_copy(dest[:, s, :], tn[s])
            d.then_inc(r_dest, 1)

            def state_step(q, k):
                if k == 0:
                    ve_.wait_ge(p_st, q + 1)
                    if from_(q, 1):
                        ve_.wait_ge(p_y, KC * q)
                        ve_.wait_ge(v_S, KC * q)
                    else:
                        ve_.wait_ge(s_zero, 1)
                else:
                    ve_.wait_ge(p_y, KC * q + 1)
                    ve_.wait_ge(v_S, KC * q + 1)
                for b in range(BATCH):
                    m = KC * b + k
                    s = ve_.scalar_tensor_tensor(
                        out=state[b][1 - k][:, :], in0=state[b][k][:, :],
                        scalar=e_tot[:, bass.ds(Q * q + m, 1)], in1=bank[7][:, P * m:P * m + P],
                        op0=ALU.mult, op1=ALU.add)
                s.then_inc(v_S, 1)

            def gate(r, w):
                for h in range(HEADS):
                    ve_.wait_ge(p_y, KC * (r + 1))
                    if from_(r, 1):
                        ve_.wait_ge(p_O, r)
                        ve_.wait_ge(s_sq, HEADS * r)
                    ve_.scalar_tensor_tensor(out=yg[:, h, :], in0=xT[w][:, h, :], scalar=d_skip[:, h:h + 1],
                                             in1=bank[5 + h][:, :], op0=ALU.mult, op1=ALU.add).then_inc(v_ye, 1)
                for h in range(HEADS):
                    ve_.wait_ge(v_ye, HEADS * r + h + 1)
                    ve_.wait_ge(s_z, HEADS * r + h + 1)
                    ve_.tensor_tensor(yg[:, h, :], yg[:, h, :], zs[w][:, h, :], ALU.mult).then_inc(v_yg, 1)

            def expert_offsets():
                link(ve_.tensor_tensor(be[0:1], block_no[:, :].unsqueeze(2).to_broadcast([1, BLOCKS, E]),
                                       en[4][0:1].unsqueeze(1).to_broadcast([1, BLOCKS, E]), ALU.is_ge))
                link(ve_.tensor_reduce(bn[0:1], be[0:1], AX.X, ALU.add))
                link(ve_.tensor_scalar(bn[0:1], bn[0:1], float(E - 1), None, ALU.min))
                ve_.memset(expert_off[:, 0:1], 0.0)
                ve_.tensor_scalar(expert_off[:, 1:], bn[0:1], float(EW), None, ALU.mult).then_inc(r_off, 1)

            def mean_square(r, w):
                ve_.wait_ge(p_O, r + 1)
                if from_(r, 2):
                    ve_.wait_ge(g_rms, r - 1)
                ve_.tensor_scalar(ms[w], bank[2][:, 0:Q], 1.0 / DI, RMS_EPS, ALU.mult, ALU.add).then_inc(v_ms, 1)

            def scan(g, w):
                i = 2 * g + w
                q, r, v = i - 1, i - 2, 1 - w
                has_r = from_(i, 2)
                has_i = before(i, QUADS)

                def scan_inputs():
                    for h in range(HEADS):
                        ve_.wait_ge(p_T, CT * q + h + 1)
                        if from_(i, 3):
                            ve_.wait_ge(p_y, KC * (q - 1))
                        ve_.tensor_tensor(xdt[v][:, :, h, :], bank[2 + h][:, :].rearrange("p (m t) -> p m t", m=Q),
                                          quad(dt_all, q)[:, :, h].unsqueeze(2).to_broadcast([P, Q, P]),
                                          ALU.mult).then_inc(v_xdt, 1)
                    if has_i:
                        halo(g, w)
                    ve_.wait_ge(p_T, CT * q + 3)
                    if from_(i, 2):
                        ve_.wait_ge(p_st, q)
                    else:
                        take_over_b(ve_)
                    for h in range(HEADS):
                        b_ = ve_.tensor_tensor(bw[:, :, h, :],
                                               bank[2][:, :].rearrange("p (m n) -> p m n", m=Q)[:, :, 0:DS],
                                               quad(w_end, q)[:, :, h].unsqueeze(2).to_broadcast([P, Q, DS]), ALU.mult)
                    b_.then_inc(v_bw, 1)

                def product_bc():
                    ve_.wait_ge(p_G, q + 1)
                    ve_.tensor_tensor(gT.rearrange("p (m t) -> p m t", m=Q),
                                      bank[3][:, :].rearrange("p (m t) -> p m t", m=Q),
                                      mid(upper[:, :], Q, P), ALU.mult).then_inc(v_gT, 1)

                if has_r:
                    gate(r, w)
                scan_inputs()
                if has_i:
                    conv_taps(g, w, (0,))
                product_bc()
                ve_.wait_ge(v_gT, q + 1)
                for n, (h, _) in enumerate(DECAY_HEADS):
                    ve_.wait_ge(s_ed, HEADS * q + n + 1)
                    if from_(i, 2):
                        ve_.wait_ge(p_y, KC * q)
                    ve_.tensor_tensor(mT[h], ed[h], gT, ALU.mult).then_inc(v_mT, 1)
                state_step(q, 0)
                if has_i:
                    conv_taps(g, w, range(1, CT), (lambda: mean_square(r, w)) if has_r else None)
                    state_step(q, 1)
                else:
                    expert_offsets()
                    mean_square(r, w)

            rolled(ve_, QUADS + 1, 4, 1, 2, scan, done=1)

            offs = []

            def fetch(g, w):
                j = R8 * g + w
                v = w % 2
                if w == 0:
                    n = min(R8, BLOCKS - j) if fixed(j) else R8
                    _, offs[:] = nc.values_load_multi_w_load_instructions(
                        expert_off[0:1, bass.ds(R8 * g + 1, n)], engines=[mybir.EngineType.DVE],
                        min_val=0, max_val=(E - 1) * EW,
                        skip_runtime_bounds_check_because="VectorE has clamped the expert to 0 .. E - 1")
                if from_(j, 2):
                    ve_.wait_ge(m_h2, j - 1)
                ve_.tensor_copy(w12[v][:, :, 0:HID], w_exp[:, bass.ds(offs[w], 2 * HID)].rearrange(
                    "p (k n) -> p k n", k=2)).then_inc(m_w, 1)

            def activate(g, w):
                j = R8 * g + w
                o = 1 - w % 2
                ve_.wait_ge(m_h2, j)
                ve_.wait_ge(m_s, j)
                if from_(j, 3):
                    ve_.wait_ge(m_o, j - 2)
                ve_.tensor_tensor(am[o], bank[5 + o][:, 0:HP], s1[o], ALU.mult).then_inc(m_a, 1)

            def moe(g, w):
                j = R8 * g + w
                if before(j, BLOCKS):
                    fetch(g, w)
                if from_(j, 1):
                    activate(g, w)

            ve_.wait_ge(r_off, 1)
            ve_.wait_ge(wts_moe, 16 * (2 + HC))
            ve_.wait_ge(s_xs, CT * QUADS)
            for v in range(2):
                ve_.memset(w12[v][:, :, HID:], 0.0)
            fetch(0, 0)
            fetch(0, 1)
            gate(QUADS - 1, 1)
            activate(0, 1)
            moe(0, 2)
            mean_square(QUADS - 1, 1)
            moe(0, 3)
            rolled(ve_, BLOCKS + 1, 4, 1, R8, moe, done=4)

            ve_.wait_ge(s_out, QUADS)
            for i in range(QUADS):
                a = ve_.tensor_tensor(quad(acc, i), quad(acc, i), quad(mamba_out, i), ALU.add)
            a.then_inc(f_acc, 1)
            ve_.wait_ge(f_acc, 1)
            ve_.wait_ge(m_yo, BLOCKS)
            results_out(ve_)

            for i in range(QUADS):
                ve_.wait_ge(y_in[i], 16 * BATCH)
                ve_.tensor_tensor(res[i], ys[i][:, :, 0, :], ys[i][:, :, 1, :], ALU.add).then_inc(f_sum, 1)
                ve_.wait_ge(f_sum, i + 1)
                ve_.tensor_tensor(res[i], res[i], quad(acc, i), ALU.add).then_inc(f_res, 1)

        @block.tensor
        def _(pe):
            pe.wait_ge(c_done, 11 + TOP_K * BATCH)

            def ln(g, w):
                i = XD * g + w
                o = (w - PE_LAG) % XD
                if before(i, QUADS):
                    pe.wait_ge(a_norm, i + 1)
                    if from_(i, XD):
                        pe.wait_ge(a_cpT, i - XD + 1)
                        pe.wait_ge(a_cpTs, i - XD + 1)
                    for m in range(Q):
                        t = pe.transpose(bank[w][:, P * m:P * m + P], xn[w][:, m, :], ident[:, :])
                    t.then_inc(a_tr, 1)
                if from_(i, PE_LAG):
                    if fixed(i) and i == PE_LAG:
                        pe.wait_ge(wts_route, 16 * 2)
                    pe.wait_ge(a_cpTs, i - PE_LAG + 1)
                    for m in range(Q):
                        t = pe.matmul(bank[7][:, bass.ds(NL * (Q * (i - PE_LAG) + m), NL)], xnTs[o][:, P * m:P * m + P],
                                      w_small[:, :], start=True, stop=True)
                    t.then_inc(a_lg, 1)

            rolled(pe, QUADS + PE_LAG, XD, PE_LAG, XD, ln)
            pe.wait_ge(wts, 128)
            pe.wait_ge(a_cpT, QUADS)
            pe.wait_ge(a_cpTs, QUADS)

            def project_conv(g, w, c):
                i = 2 * g + w
                if c < 2 and from_(i, 1):
                    pe.wait_ge(s_z, HEADS * (i - 1) + 2 - c)
                if c == 2:
                    pe.wait_ge(s_pre, CT * i + 1)
                pe.matmul(bank[c % 2][:, :], w_in[:, DI + P * c:DI + P * c + P], xnT[:, bass.ds(W * i, W)],
                          start=True, stop=True).then_inc(p_pre, 1)

            def project_z(g, w, h):
                i = 2 * g + w
                pe.wait_ge(s_pre, CT * i + 2 + h)
                pe.matmul(bank[1 - h][:, :], w_in[:, P * h:P * h + P], xnT[:, bass.ds(W * i, W)],
                          start=True, stop=True).then_inc(p_z, 1)

            for c in range(CT):
                project_conv(0, 0, c)
            for h in range(HEADS):
                project_z(0, 0, h)
            pe.wait_ge(r_mask, 1)
            mask = VT[0].rearrange("p e r -> p (e r)")
            pe.matmul(bank[5][:, 0:E * TILES], earlier[:, :], mask, start=True, stop=True)
            pe.matmul(bank[6][:, 0:E * TILES], ones[:, :], mask, start=True, stop=True).then_inc(r_cnt, 1)
            pe.wait_ge(r_a, 1)
            C2 = TILES * HEADS
            a2 = a_all[:, :, :].rearrange("p r h -> p (r h)")
            for k, t in enumerate((upper, after, ones)):
                s = pe.matmul(bank[3][:, C2 * k:C2 * k + C2], t[:, :], a2, start=True, stop=True)
            s.then_inc(r_cum, 1)
            pe.wait_ge(r_ecum, 1)
            pe.transpose(bank[2][0:C2, 0:P], ecum.rearrange("p r h -> p (r h)"), ident[:, :]).then_inc(r_ecT, 1)
            pe.wait_ge(r_tot, 1)
            pe.wait_ge(r_ecS, 1)

            def scan(g, w):
                i = 2 * g + w
                q, r, v = i - 1, i - 2, 1 - w
                has_q = from_(i, 1) and before(i, QUADS + 1)

                def decays(n):
                    h, to = DECAY_HEADS[n]
                    pe.wait_ge(g_aU, HEADS * q + n + 1)
                    if from_(i, 2) and n == 0:
                        pe.wait_ge(v_S, KC * q)
                    if from_(i, 3) and n == 1:
                        pe.wait_ge(s_out, r)
                    pe.matmul(to[:, :], after[:, :], aU[:, h, :], start=True, stop=True).then_inc(p_D, 1)

                if has_q:
                    decays(0)
                    for h in range(HEADS):
                        pe.wait_ge(s_xs, CT * q + h + 1)
                        if from_(i, 2):
                            pe.wait_ge(v_bw if h == 0 else v_gT, q)
                        if from_(i, 3) and h == 0:
                            pe.wait_ge(v_ms, r)
                        for m in range(Q):
                            t = pe.transpose(bank[2 + h][:, P * m:P * m + P], xT[v][:, h, P * m:P * m + P], ident[:, :])
                        t.then_inc(p_T, 1)
                if before(i, QUADS):
                    project_conv(g, w, 0)
                if has_q:
                    decays(1)
                if before(i, QUADS):
                    project_conv(g, w, 1)
                if has_q:
                    pe.wait_ge(s_xs, CT * q + 3)
                    pe.wait_ge(v_xdt, HEADS * q + 1)
                    for m in range(Q):
                        t = pe.transpose(bank[2][:, P * m:P * m + P], bcT[v][:, P * m:P * m + P], ident[:, :])
                    t.then_inc(p_T, 1)
                    pe.wait_ge(c_in[v], 16 * HEADS * (g + w))
                    pe.wait_ge(v_xdt, HEADS * q + 2)
                    for m in range(Q):
                        t = pe.matmul(bank[3][:, P * m:P * m + P], bcT[v][0:DS, P * m:P * m + P],
                                      cd[v][0:DS, P * m:P * m + P], start=True, stop=True)
                    t.then_inc(p_G, 1)
                if before(i, QUADS):
                    project_conv(g, w, 2)
                if before(i, QUADS):
                    project_z(g, w, 0)
                if has_q:
                    pe.wait_ge(v_xdt, HEADS * (q + 1))
                    pe.wait_ge(v_bw, q + 1)
                    pe.wait_ge(s_ed, HEADS * q + 1)
                    for m in range(Q):
                        for h in range(HEADS):
                            t = pe.matmul(bank[7][DS * h:DS * h + DS, P * m:P * m + P], bw[:, m, h, :],
                                          xdt[v][:, m, h, :], start=True, stop=True)
                    t.then_inc(p_st, 1)
                if from_(i, 2):
                    pe.wait_ge(v_yg, HEADS * (r + 1))
                    pe.wait_ge(r_wo, 1)
                    pe.wait_ge(g_sq, r + 1)
                    if has_q:
                        pe.wait_ge(s_ed, HEADS * q + 2)
                        pe.wait_ge(v_bw, q + 1)
                    else:
                        pe.wait_ge(m_xg, 3)
                        pe.wait_ge(s_out, r)
                    for m in range(Q):
                        for h in range(HEADS):
                            pe.matmul(bank[4][:, P * m:P * m + P], yg[:, h, P * m:P * m + P], w_out[:, h, :],
                                      start=(h == 0), stop=(h == HEADS - 1))
                        t = pe.matmul(bank[2][:, m:m + 1], sq_sum[:, P * m:P * m + P], ones[:, 0:1],
                                      start=True, stop=True)
                    t.then_inc(p_O, 1)
                if before(i, QUADS):
                    project_z(g, w, 1)
                if has_q:
                    pe.wait_ge(v_mT, HEADS * (q + 1))
                    pe.wait_ge(g_ce, q + 1)
                    if from_(i, 2):
                        pe.wait_ge(v_ye, HEADS * q)
                    else:
                        pe.wait_ge(r_dest, 1)
                        pe.wait_ge(s_zero, 1)
                    for k in range(KC):
                        if k > 0:
                            pe.wait_ge(v_S, KC * q + k)
                        elif from_(i, 2):
                            pe.wait_ge(v_S, KC * q)
                        for b in range(BATCH):
                            m = KC * b + k
                            for h in range(HEADS):
                                o = bank[5 + h][:, P * m:P * m + P]
                                pe.matmul(o, xdt[v][:, m, h, :], mT[h][:, P * m:P * m + P], start=True, stop=False)
                                t = pe.matmul(o, state[b][k][DS * h:DS * h + DS, :],
                                              ce[DS * h:DS * h + DS, P * m:P * m + P], start=False, stop=True)
                        t.then_inc(p_y, 1)

            rolled(pe, QUADS + 1, 4, 1, 2, scan, done=1)

            pe.wait_ge(wts_moe, 16 * (2 + HC))
            pe.wait_ge(r_off, 1)

            def turn_rows(g, w):
                j = R8 * g + w
                pe.wait_ge(m_in[w], 16 * (g + 1))
                if from_(j, 1):
                    pe.wait_ge(m_xg, j)
                if fixed(j) and j == 3:
                    pe.wait_ge(v_ms, QUADS)
                pe.transpose(bank[2][:, 0:P], xin[w][:, 0:D], ident[:, :]).then_inc(m_T, 1)

            pe.wait_ge(v_bw, QUADS)
            pe.wait_ge(v_gT, QUADS)
            pe.wait_ge(v_ms, QUADS - 1)
            pe.wait_ge(s_z, HEADS * QUADS)
            turn_rows(0, 0)

            def hidden(to, x, weights):
                for k in range(HC):
                    t = pe.matmul(to[:, P * k:P * k + P], weights[:, P * k:P * k + P], x, start=True, stop=True)
                return t

            offs = []

            def moe(g, w):
                j = R8 * g + w
                v = w % 2
                if w == 0:
                    n = min(R8, BLOCKS + 1 - j) if fixed(j) else R8
                    _, offs[:] = nc.values_load_multi_w_load_instructions(
                        expert_off[0:1, bass.ds(R8 * g, n)], engines=[mybir.EngineType.PE],
                        min_val=0, max_val=(E - 1) * EW,
                        skip_runtime_bounds_check_because="VectorE has clamped the expert to 0 .. E - 1")
                if before(j, BLOCKS):
                    pe.wait_ge(m_xg, j + 1)
                    if from_(j, 2):
                        pe.wait_ge(m_s, j - 1)
                    pe.wait_ge(m_w, j + 1)
                    hidden(bank[v], xg[v], w12[v][:, 0]).then_inc(m_h1, 1)
                    if before(j + 1, BLOCKS):
                        turn_rows(g if w < R8 - 1 else g + 1, (w + 1) % R8)
                    if from_(j, 2):
                        pe.wait_ge(m_a, j - 1)
                    elif j == 0:
                        pe.wait_ge(v_ye, HEADS * QUADS)
                    hidden(bank[5 + v], xg[v], w12[v][:, 1]).then_inc(m_h2, 1)
                if from_(j, 1):
                    off = offs[w]
                    pe.wait_ge(m_a, j)
                    if from_(j, 2):
                        pe.wait_ge(m_yo, j - 1)
                    for k in range(HC):
                        t = pe.matmul(bank[3][:, 0:D], am[1 - v][:, P * k:P * k + P],
                                      w_exp[:, bass.ds(off + 2 * HID + D * k, D)], start=(k == 0), stop=(k == HC - 1))
                    t.then_inc(m_o, 1)

            moe(0, 0)
            moe(0, 1)
            scan(QUADS // 2, 1)
            rolled(pe, BLOCKS + 1, 3, 2, R8, moe, done=2)


def kernel(**inputs):
    import numpy as np
    import concourse.bacc as bacc
    from concourse.bass_utils import run_bass_kernel_spmd

    a = {k: np.asarray(v) for k, v in inputs.items()}
    conv_w = a["L0_attn_conv_w"]
    laid = {
        "u": a["L0_attn_u"],
        "in_projT": a["L0_attn_in_proj_w"].T,
        "conv_w": conv_w.reshape(-1, 128, conv_w.shape[2]).transpose(1, 0, 2),
        "conv_b": a["L0_attn_conv_b"].reshape(-1, 128).T,
        "dt_bias": a["L0_attn_dt_bias"],
        "A_log": a["L0_attn_A_log"],
        "D_param": a["L0_attn_D_param"],
        "norm_w": a["L0_attn_norm_w"].reshape(-1, 128).T,
        "out_projT": a["L0_attn_out_proj_w"].T,
        "gateT": a["L0_ffn_gate_w"].T,
        "w1T": a["L0_ffn_w1"].transpose(2, 0, 1),
        "w2T": a["L0_ffn_w2"].transpose(2, 0, 1),
        "w3T": a["L0_ffn_w3"].transpose(2, 0, 1),
    }
    nc = bacc.Bacc("TRN2", target_bir_lowering=False, num_devices=1)
    arrays, args = {}, []
    for name, x in laid.items():
        x = np.ascontiguousarray(x)
        arrays["in_" + name] = x
        args.append(nc.dram_tensor("in_" + name, x.shape, mybir.dt.from_np(x.dtype), kind="ExternalInput").ap())
    out = nc.dram_tensor("out_0", laid["u"].shape, F32, kind="ExternalOutput").ap()
    build(nc, *args, out)
    r = run_bass_kernel_spmd(nc, [arrays], core_ids=[0])
    return r.results[0]["out_0"]
```
